# Optimizing a Trainium2 kernel written in Bass

```python
import numpy as np
import jax
import jax.numpy as jnp

def _softmax(x, axis=-1):
    return jax.nn.softmax(x, axis=axis)

def _gelu(x):
    return jax.nn.gelu(x, approximate=True)

def _silu(x):
    return jax.nn.silu(x)

def _sigmoid(x):
    return jax.nn.sigmoid(x)

def _layernorm(x, axis=-1, eps=1e-05):
    m = jnp.mean(x, axis=axis, keepdims=True)
    v = jnp.var(x, axis=axis, keepdims=True)
    return (x - m) / jnp.sqrt(v + eps)

def _scatter_add(tgt, idx, src, axis=0):
    return tgt.at[idx].add(src)

def _segment_sum(src, seg, n):
    return jax.ops.segment_sum(src, seg, n)
kernel_name = 'mk_decoder_preln_d1_seqx_r8_9f3df1'

def setup_inputs(seed: int=0):
    np.random.seed(seed)
    _w = jnp.asarray

    def _rec_inputs():
        import jax
        import jax.numpy as jnp
        _rk = jax.random.key(seed)
        x = -0.0005207 + 1.001 * jax.random.normal(jax.random.fold_in(_rk, 1), (16, 64, 512), jnp.float32)
        _lenS = 64 - jax.random.randint(jax.random.fold_in(_rk, 7), (16,), 0, max(1, 64 // 4) + 1, jnp.int32)
        _lenS2 = 64 - jax.random.randint(jax.random.fold_in(_rk, 8), (16,), 0, max(1, 64 // 4) + 1, jnp.int32)
        _ctx_4096P = jax.random.normal(jax.random.fold_in(_rk, 11), (16, 16, 512), jnp.float32)
        _ctx_4096c = jax.random.dirichlet(jax.random.fold_in(_rk, 511), 0.3 * jnp.ones((16,), jnp.float32), (16, 64))
        _ctx_4096t = jnp.einsum('bsk,bkd->bsd', _ctx_4096c, _ctx_4096P)
        _ctx_4096t = _ctx_4096t * jax.lax.rsqrt(jnp.mean(jnp.square(_ctx_4096t)) + 1e-12) * 0.953939
        ctx_4096 = -0.00010331 + 0.999899 * (_ctx_4096t + 0.3 * jax.random.normal(jax.random.fold_in(_rk, 611), (16, 64, 512), jnp.float32))
        return (x, ctx_4096)
    x, ctx_4096 = _rec_inputs()

    def _L0_attn_setup():
        import jax, jax.numpy as jnp
        import numpy as np
        B, S, HID = (2, 512, 512)
        H, HKV, D = (32, 8, 128)
        G = H // HKV
        EPS = 1e-06

        def _reference_tuple_inner(hidden_states, Wq, bq, Wk, bk, Wv, bv, Wo, M, z):
            b, s, _ = hidden_states.shape
            q = (hidden_states @ Wq.T + bq).reshape(b, s, H, D)
            k = (hidden_states @ Wk.T + bk).reshape(b, s, HKV, D)
            v = (hidden_states @ Wv.T + bv).reshape(b, s, HKV, D)
            sig_q = jax.nn.elu(q) + 1.0
            sig_k = jax.nn.elu(k) + 1.0
            q_sel = sig_q[:, :, ::G, :]
            num = jnp.einsum('bshd,hde->bshe', q_sel, M)
            den = jnp.einsum('bshd,hd->bsh', q_sel, z)[..., None] + EPS
            retrieved = num / den
            out_heads = jnp.repeat(retrieved, G, axis=2)
            output = out_heads.reshape(b, s, H * D) @ Wo.T
            M_new = M + jnp.einsum('bshd,bshe->hde', sig_k, v)
            z_new = z + sig_k.sum(axis=(0, 1))
            return (output, M_new, z_new)
        key = jax.random.key(seed)
        ks = jax.random.split(key, 10)
        s = 0.02
        return {'hidden_states': jax.random.normal(ks[0], (B, S, HID), jnp.float32), 'Wq': jax.random.normal(ks[1], (H * D, HID), jnp.float32) * s, 'bq': jnp.zeros((H * D,), jnp.float32), 'Wk': jax.random.normal(ks[2], (HKV * D, HID), jnp.float32) * s, 'bk': jnp.zeros((HKV * D,), jnp.float32), 'Wv': jax.random.normal(ks[3], (HKV * D, HID), jnp.float32) * s, 'bv': jnp.zeros((HKV * D,), jnp.float32), 'Wo': jax.random.normal(ks[4], (HID, H * D), jnp.float32) * s, 'M': jax.random.normal(ks[5], (HKV, D, D), jnp.float32), 'z': jax.random.uniform(ks[6], (HKV, D), jnp.float32) * 100.0 + 1.0}
    _L0_attn_all = _L0_attn_setup()
    _L0_attn_in = {k: v for k, v in _L0_attn_all.items() if k in ('Wq', 'bq', 'Wk', 'bk', 'Wv', 'bv', 'Wo', 'M', 'z')}
    del _L0_attn_all

    def _L0_xattn_setup():
        import jax, jax.numpy as jnp
        import numpy as np
        import math
        HIDDEN = 512
        N_HEADS = 32
        HEAD_DIM = 128
        N_KV_HEADS = 4
        N_GROUPS = N_HEADS // N_KV_HEADS
        key = jax.random.key(seed)
        ks = jax.random.split(key, 6)
        B, NL, S = (8, 64, 512)
        latents = jax.random.normal(ks[0], (B, NL, HIDDEN), dtype=jnp.float32)
        context = jax.random.normal(ks[1], (B, S, HIDDEN), dtype=jnp.float32)
        scale = 1.0 / math.sqrt(HIDDEN)
        Wq = jax.random.normal(ks[2], (HIDDEN, N_HEADS * HEAD_DIM), dtype=jnp.float32) * scale
        Wk = jax.random.normal(ks[3], (HIDDEN, N_KV_HEADS * HEAD_DIM), dtype=jnp.float32) * scale
        Wv = jax.random.normal(ks[4], (HIDDEN, N_KV_HEADS * HEAD_DIM), dtype=jnp.float32) * scale
        Wo = jax.random.normal(ks[5], (N_HEADS * HEAD_DIM, HIDDEN), dtype=jnp.float32) * scale
        return {'latents': latents, 'context': context, 'Wq': Wq, 'Wk': Wk, 'Wv': Wv, 'Wo': Wo}
    _L0_xattn_all = _L0_xattn_setup()
    _L0_xattn_in = {k: v for k, v in _L0_xattn_all.items() if k in ('Wq', 'Wk', 'Wv', 'Wo')}
    del _L0_xattn_all

    def _L0_ffn_setup():
        import jax, jax.numpy as jnp
        import numpy as np
        K_TOP = 8
        key = jax.random.key(seed)
        k1, k2, k3 = jax.random.split(key, 3)
        B, S, H, E = (4, 512, 512, 64)
        hidden_states = jax.random.normal(k1, (B, S, H), dtype=jnp.float32)
        router_weight = jax.random.normal(k2, (E, H), dtype=jnp.float32)
        router_bias = jnp.zeros((E,), dtype=jnp.float32)
        expert_bias = jax.random.normal(k3, (E, H), dtype=jnp.float32) * 0.1
        return {'hidden_states': hidden_states, 'router_weight': router_weight, 'router_bias': router_bias, 'expert_bias': expert_bias}
    _L0_ffn_all = _L0_ffn_setup()
    _L0_ffn_in = {k: v for k, v in _L0_ffn_all.items() if k in ('router_weight', 'router_bias', 'expert_bias')}
    del _L0_ffn_all
    return {'x': x, 'ctx_4096': ctx_4096, 'L0_attn_Wq': _L0_attn_in['Wq'], 'L0_attn_bq': _L0_attn_in['bq'], 'L0_attn_Wk': _L0_attn_in['Wk'], 'L0_attn_bk': _L0_attn_in['bk'], 'L0_attn_Wv': _L0_attn_in['Wv'], 'L0_attn_bv': _L0_attn_in['bv'], 'L0_attn_Wo': _L0_attn_in['Wo'], 'L0_attn_M': _L0_attn_in['M'], 'L0_attn_z': _L0_attn_in['z'], 'L0_xattn_Wq': _L0_xattn_in['Wq'], 'L0_xattn_Wk': _L0_xattn_in['Wk'], 'L0_xattn_Wv': _L0_xattn_in['Wv'], 'L0_xattn_Wo': _L0_xattn_in['Wo'], 'L0_ffn_router_weight': _L0_ffn_in['router_weight'], 'L0_ffn_router_bias': _L0_ffn_in['router_bias'], 'L0_ffn_expert_bias': _L0_ffn_in['expert_bias']}

def reference(x, ctx_4096, L0_attn_Wq, L0_attn_bq, L0_attn_Wk, L0_attn_bk, L0_attn_Wv, L0_attn_bv, L0_attn_Wo, L0_attn_M, L0_attn_z, L0_xattn_Wq, L0_xattn_Wk, L0_xattn_Wv, L0_xattn_Wo, L0_ffn_router_weight, L0_ffn_router_bias, L0_ffn_expert_bias):
    import jax
    import jax.numpy as jnp

    def _L0_attn_ref(hidden_states, Wq, bq, Wk, bk, Wv, bv, Wo, M, z):
        import jax, jax.numpy as jnp
        import numpy as np
        B, S, HID = (2, 512, 512)
        H, HKV, D = (32, 8, 128)
        G = H // HKV
        EPS = 1e-06

        def _reference_tuple_inner(hidden_states, Wq, bq, Wk, bk, Wv, bv, Wo, M, z):
            b, s, _ = hidden_states.shape
            q = (hidden_states @ Wq.T + bq).reshape(b, s, H, D)
            k = (hidden_states @ Wk.T + bk).reshape(b, s, HKV, D)
            v = (hidden_states @ Wv.T + bv).reshape(b, s, HKV, D)
            sig_q = jax.nn.elu(q) + 1.0
            sig_k = jax.nn.elu(k) + 1.0
            q_sel = sig_q[:, :, ::G, :]
            num = jnp.einsum('bshd,hde->bshe', q_sel, M)
            den = jnp.einsum('bshd,hd->bsh', q_sel, z)[..., None] + EPS
            retrieved = num / den
            out_heads = jnp.repeat(retrieved, G, axis=2)
            output = out_heads.reshape(b, s, H * D) @ Wo.T
            M_new = M + jnp.einsum('bshd,bshe->hde', sig_k, v)
            z_new = z + sig_k.sum(axis=(0, 1))
            return (output, M_new, z_new)
        return _reference_tuple_inner(hidden_states, Wq, bq, Wk, bk, Wv, bv, Wo, M, z)[0]

    def _L0_xattn_ref(latents, context, Wq, Wk, Wv, Wo):
        import jax, jax.numpy as jnp
        import numpy as np
        import math
        HIDDEN = 512
        N_HEADS = 32
        HEAD_DIM = 128
        N_KV_HEADS = 4
        N_GROUPS = N_HEADS // N_KV_HEADS
        b, q_len, _ = latents.shape
        kv_len = q_len + context.shape[1]
        hidden_states = jnp.concatenate([context, latents], axis=1)
        q = (latents @ Wq).reshape(b, q_len, N_KV_HEADS, N_GROUPS, HEAD_DIM)
        k = (hidden_states @ Wk).reshape(b, kv_len, N_KV_HEADS, HEAD_DIM)
        v = (hidden_states @ Wv).reshape(b, kv_len, N_KV_HEADS, HEAD_DIM)
        scale = 1.0 / math.sqrt(HEAD_DIM)
        scores = jnp.einsum('bqhgd,bkhd->bhgqk', q, k) * scale
        attn = jax.nn.softmax(scores.astype(jnp.float32), axis=-1).astype(q.dtype)
        out = jnp.einsum('bhgqk,bkhd->bqhgd', attn, v)
        out = out.reshape(b, q_len, N_HEADS * HEAD_DIM)
        return out @ Wo

    def _L0_ffn_ref(hidden_states, router_weight, router_bias, expert_bias):
        import jax, jax.numpy as jnp
        import numpy as np
        K_TOP = 8
        B, S, H = hidden_states.shape
        E = router_weight.shape[0]
        T = B * S
        flat = hidden_states.reshape(T, H)
        logits = jnp.einsum('th,eh->te', flat, router_weight) + router_bias
        scores = jax.nn.softmax(logits, axis=-1)
        topk_w, topk_idx = jax.lax.top_k(scores, K_TOP)
        w_sum = topk_w.sum(axis=-1, keepdims=True)
        w_dense = jnp.zeros((T, E), dtype=scores.dtype).at[jnp.arange(T)[:, None], topk_idx].add(topk_w)
        bias_mix = jnp.einsum('te,eh->th', w_dense, expert_bias)
        out = flat * w_sum + bias_mix
        return out.reshape(B, S, H)
    x = x + _L0_attn_ref(_layernorm(x, axis=-1), L0_attn_Wq, L0_attn_bq, L0_attn_Wk, L0_attn_bk, L0_attn_Wv, L0_attn_bv, L0_attn_Wo, L0_attn_M, L0_attn_z)
    x = x + _L0_xattn_ref(_layernorm(x, axis=-1), ctx_4096, L0_xattn_Wq, L0_xattn_Wk, L0_xattn_Wv, L0_xattn_Wo)
    x = x + _L0_ffn_ref(_layernorm(x, axis=-1), L0_ffn_router_weight, L0_ffn_router_bias, L0_ffn_expert_bias)
    return x

_drawn_inputs = setup_inputs


def setup_inputs(seed=0):
    import zlib

    import numpy as np

    out = dict(_drawn_inputs(seed))
    spreads = {'L0_attn_bq': (0.0, 2.0),
     'L0_attn_bk': (0.0, 0.1),
     'L0_attn_bv': (0.0, 0.1),
     'L0_ffn_router_bias': (0.0, 2.0)}
    factors = {'L0_attn_Wq': 183.504, 'L0_attn_Wo': 64.0, 'L0_attn_M': 64.0, 'L0_attn_z': 200.0}
    for name, (base, spread) in spreads.items():
        noise = np.random.default_rng([zlib.crc32(name.encode()), seed]).standard_normal(out[name].shape)
        drawn = base * np.exp(spread * noise) if base else spread * noise
        out[name] = jnp.asarray(drawn.astype(out[name].dtype))
    for name, factor in factors.items():
        out[name] = (out[name] * factor).astype(out[name].dtype)
    return out
```

```python
import concourse.bass as bass
import numpy as np
from concourse import mybir
from contextlib import ExitStack


def decoder_layer(
    nc: bass.Bass,
    x_in: bass.AP,
    ctx_in: bass.AP,
    attn_Wq: bass.AP,
    attn_bq: bass.AP,
    attn_Wo: bass.AP,
    attn_M: bass.AP,
    attn_z: bass.AP,
    x_Wq: bass.AP,
    x_Wk: bass.AP,
    x_Wv: bass.AP,
    x_Wo: bass.AP,
    router_w: bass.AP,
    router_b: bass.AP,
    expert_b: bass.AP,
    out: bass.AP,
):
    F = mybir.dt.float32
    R = mybir.dt.float32r
    ALU = mybir.AluOpType
    ACT = mybir.ActivationFunctionType
    AX = mybir.AxisListType.X

    P = 128
    B, S, D = x_in.shape
    NT = B * S // P
    KC = D // P
    NTOK = B * S
    HALF = NTOK // 2
    H = attn_Wq.shape[0] // P
    MH = attn_M.shape[0]
    GREP = H // MH
    KV = x_Wk.shape[1] // P
    GH = H // KV
    NE = router_w.shape[0]
    SCALE = float(P) ** -0.5
    LN_EPS = 1e-5
    DEN_EPS = 1e-6
    assert (NT, KC, H, MH, KV, GH, NE) == (8, 4, 32, 8, 4, 8, 64)

    x_tiles = x_in.rearrange("b s d -> (b s) d").rearrange("(t p) d -> p t d", p=P)
    ctx_tiles = ctx_in.rearrange("b s d -> (b s) d").rearrange("(t p) d -> p t d", p=P)
    out_tiles = out.rearrange("b s d -> (b s) d").rearrange("(t p) d -> p t d", p=P)
    wqa_heads = attn_Wq.rearrange("(m g p) k -> g p m k", g=GREP, p=P)[0]
    bq_rows = attn_bq.rearrange("(m g p) -> g m p", g=GREP, p=P)[0]
    woa_heads = attn_Wo.rearrange("(o p) (m c) -> m p o c", p=P, m=MH)
    mem_heads = attn_M.rearrange("m d e -> d m e")
    wk_rows = x_Wk.rearrange("(k p) n -> p k n", p=P)
    wv_rows = x_Wv.rearrange("(k p) n -> p k n", p=P)
    wq_rows = x_Wq.rearrange("(k p) n -> p k n", p=P)
    wo_rows = x_Wo.rearrange("(h p) n -> p h n", p=P)

    keys_dram = nc.dram_tensor("keys_dram", (KV, 2, P, NTOK), F, kind="Internal").ap()
    vals_dram = nc.dram_tensor("vals_dram", (2, NTOK, KV * P), F, kind="Internal").ap()

    ctx = ExitStack()
    with ctx:
        def sb(name, shape, dt=F, stack=ctx):
            return stack.enter_context(nc.sbuf_tensor(name, shape, dt))

        def sem(name):
            return ctx.enter_context(nc.semaphore(name))

        resid = sb("resid", [P, NT, D])
        xnT = sb("xnT", [P, 2, KC, NTOK], R)
        regA = sb("regA", [P, 2, 4096], R)
        regC = sb("regC", [P, 2, 4096], R)
        raw16 = sb("raw16", [P, 4096])
        ident = sb("ident", [P, P])
        neg_half = sb("neg_half", [P, 1])
        bz = sb("bz", [P, 2 * MH])
        rden = sb("rden", [P, 2, 4, MH])
        stats = sb("stats", [P, 6])
        meanvar = sb("meanvar", [P, 2])
        vareps = sb("vareps", [P, 1])
        rstd = sb("rstd", [P, 1])
        negmax = sb("negmax", [P, 2, 4])
        rowsum = sb("rowsum", [P, 2, 4])
        rrow = sb("rrow", [P, 2, 4])

        first = ExitStack()
        regB = sb("regB", [P, 2, 4096], R, first)
        rawk = sb("rawk", [P, 4096], F, first)
        sig = sb("sig", [P, 2, HALF], F, first)
        qneg = sb("qneg", [P, HALF], F, first)
        qpos = sb("qpos", [P, HALF], F, first)
        wofold = sb("wofold", [P, 2, KC, P], F, first)
        wofT = sb("wofT", [P, 2, D], R, first)
        memT = sb("memT", [P, 2, P], R, first)
        mem = sb("mem", [P, MH, P], F, first)
        xn = sb("xn", [P, 2, D], F, first)
        kvout = sb("kvout", [P, 2, D], F, first)
        first.close()

        second = ExitStack()
        qT = sb("qT", [P, 2, 8, GH, S], F, second)
        oT = sb("oT", [P, 2, 2, GH, P], R, second)
        wq_raw = sb("wq_raw", [P, KC, 2 * P], F, second)
        k_ring = sb("k_ring", [P, 4, 2, P], F, second)
        v_raw = sb("v_raw", [P, 2, 2, P], F, second)
        v_ring = sb("v_ring", [P, 2, 2, 2, P], R, second)
        probs = sb("probs", [P, 2, 4, P], F, second)
        pT = sb("pT", [P, 2, 2, 4 * P], R, second)
        second.close()
        bank = [ctx.enter_context(nc.psum_tensor(f"bank{i}", [P, 512], F)) for i in range(8)]

        hi_lo = (0, 1)
        ctxT = regA[:, :, :].rearrange("p a (k n) -> p a k n", k=KC)
        sigT = regA[:, :, :].rearrange("p a (m n) -> p a m n", m=MH)
        wq = regA[:, :, :].rearrange("p a (h k n) -> p a h k n", h=GH, k=KC)
        wkv1 = regB[:, :, :].rearrange("p a (w k n) -> p a w k n", w=2, k=KC)
        memwo = regB[:, :, :].rearrange("p a (m n) -> p a m n", m=MH)
        wqaT = regC[:, :, :].rearrange("p a (m k n) -> p a m k n", m=MH, k=KC)
        wkv2 = regC[:, :, :].rearrange("p a (w k n) -> p a w k n", w=2, k=KC)
        wo = regC[:, :, :].rearrange("p a (h n) -> p a h n", h=GH)
        ctx_raw = raw16[:, :].rearrange("p (t n) -> p t n", t=NT)
        woa_raw = raw16[:, :].rearrange("p (r o g n) -> p r o g n", r=2, o=KC, g=GREP)
        wo_raw = raw16[:, :].rearrange("p (h n) -> p h n", h=GH)
        wkv_raw = rawk[:, :].rearrange("p (w k n) -> p w k n", w=2, k=KC)
        wqa_raw = rawk[:, :].rearrange("p (m n) -> p m n", m=MH)
        bz_rows = qneg[0:2 * MH, 0:P]
        e_xn = raw16[:, 0:2 * D].rearrange("p (r n) -> p r n", r=2)
        e_xnT = raw16[:, 2 * D:4 * D].rearrange("p (r k n) -> p r k n", r=2, k=KC)
        e_out = raw16[:, 4 * D:6 * D].rearrange("p (r n) -> p r n", r=2)
        rout_rows = raw16[0:NE, 5 * D:6 * D]
        expert = raw16[0:NE, 6 * D:7 * D]
        routT = raw16[:, 7 * D:7 * D + KC * NE].rearrange("p (k n) -> p k n", k=KC)
        wq_flat = wq_raw[:, :, :].rearrange("p k n -> p (k n)")
        small = wq_flat[:, 0:10 * NE].rearrange("p (r w n) -> p r w n", r=2, w=5)
        e_wT = wq_flat[0:NE, 10 * NE:10 * NE + 2 * P].rearrange("p (r n) -> p r n", r=2)
        rout_b = wq_flat[:, 14 * NE:15 * NE]
        top = wq_flat[:, 15 * NE:16 * NE].rearrange("p (r w n) -> p r w n", r=2, w=4)

        ctx_loaded = [sem(f"ctx_loaded{i}") for i in range(4)]
        wkv_loaded = [sem("wk_loaded"), sem("wv_loaded")]
        x_loaded = [sem(f"x_loaded{i}") for i in range(4)]
        bz_loaded = sem("bz_loaded")
        mem_loaded = sem("mem_loaded")
        wqa_loaded = [sem(f"wqa_loaded{i}") for i in range(4)]
        woa_loaded = [sem(f"woa_loaded{i}") for i in range(2)]
        expert_loaded = sem("expert_loaded")
        consts_set = sem("consts_set")
        tr_done = sem("tr_done")
        tr_hi = sem("tr_hi")
        tr_used = sem("tr_used")
        mm_done = sem("mm_done")
        mm_act = sem("mm_act")
        mm_dve = sem("mm_dve")
        wkv_hi = sem("wkv_hi")
        wkv_lo = sem("wkv_lo")
        kv_written = [sem("kv_written0"), sem("kv_written1")]
        dve_step = sem("dve_step")
        var_ready = sem("var_ready")
        rstd_ready = sem("rstd_ready")
        xn_ready = sem("xn_ready")
        qexp_ready = sem("qexp_ready")
        qpos_ready = sem("qpos_ready")
        sig_ready = sem("sig_ready")
        sig_hi = sem("sig_hi")
        sig_lo = sem("sig_lo")
        den_done = sem("den_done")
        rden_ready = sem("rden_ready")
        fold_half = sem("fold_half")
        fold_done = sem("fold_done")
        y_done = sem("y_done")
        y_used = sem("y_used")
        k_loaded = [sem(f"k_loaded{i}") for i in range(4)]
        v_loaded = [sem(f"v_loaded{i}") for i in range(2)]
        wq_loaded = sem("wq_loaded")
        wo_loaded = sem("wo_loaded")
        wq_hi = sem("wq_hi")
        wq_lo = sem("wq_lo")
        wo_hi = sem("wo_hi")
        wo_lo = sem("wo_lo")
        wo_used = sem("wo_used")
        v_hi = sem("v_hi")
        v_lo = sem("v_lo")
        q_done = sem("q_done")
        q_saved = sem("q_saved")
        scores_done = sem("scores_done")
        negmax_ready = sem("negmax_ready")
        rrow_ready = sem("rrow_ready")
        exp_done = sem("exp_done")
        probs_ready = sem("probs_ready")
        pT_done = sem("pT_done")
        pT_hi = sem("pT_hi")
        pT_lo = sem("pT_lo")
        pv_done = sem("pv_done")
        oT_hi = sem("oT_hi")
        oT_lo = sem("oT_lo")
        proj_done = sem("proj_done")
        proj_added = sem("proj_added")
        routT_done = sem("routT_done")
        routT_ready = sem("routT_ready")
        e_xn_ready = sem("e_xn_ready")
        e_tr_done = sem("e_tr_done")
        e_xnT_ready = sem("e_xnT_ready")
        logits_done = sem("logits_done")
        logits_saved = sem("logits_saved")
        e_max_ready = sem("e_max_ready")
        e_exp_done = sem("e_exp_done")
        e_w_ready = sem("e_w_ready")
        e_wT_done = sem("e_wT_done")
        e_wT_ready = sem("e_wT_ready")
        mix_done = sem("mix_done")
        e_out_ready = sem("e_out_ready")
        out_written = [sem("out_written0"), sem("out_written1")]

        TR_CTX, TR_X, TR_BZ, TR_WQA, TR_MEM, TR_X2 = 0, 8, 16, 17, 25, 41
        MM_KCTX, MM_VCTX, MM_Q0, MM_MW, MM_Q1, MM_VLAT, MM_KLAT, MM_XQ = 0, 8, 16, 24, 32, 40, 48, 56

        def tr_hi_count(k):
            return k + 1 - (k >= TR_BZ)

        def mm_dve_count(k):
            return min(max(k + 1 - MM_Q0, 0), 24)

        def tr_bank(k):
            return bank[k % 2]

        def mm_bank(k):
            return bank[2 + k % 2]

        den_bank = bank[4]

        def y_bank(k):
            return bank[5 + k % 3]

        PARTS = ((0, 0), (0, 1), (1, 0))

        block = ctx.enter_context(nc.Block())

        @block.sync
        def _(sp):
            for i in range(4):
                sp.dma_start(ctx_raw[:, 2 * i:2 * i + 2, :], ctx_tiles[:, 2 * i:2 * i + 2, :])\
                  .then_inc(ctx_loaded[i], 16)
            for w, rows in enumerate((wk_rows, wv_rows)):
                sp.dma_start(wkv_raw[:, w, :, :], rows).then_inc(wkv_loaded[w], 16)
            for i in range(4):
                sp.dma_start(resid[:, 2 * i:2 * i + 2, :], x_tiles[:, 2 * i:2 * i + 2, :])\
                  .then_inc(x_loaded[i], 16)
            sp.dma_start(bz_rows[0:MH, :], bq_rows).then_inc(bz_loaded, 16)
            sp.dma_start(bz_rows[MH:2 * MH, :], attn_z).then_inc(bz_loaded, 16)
            sp.dma_start(mem[:, :, :], mem_heads).then_inc(mem_loaded, 16)
            sp.wait_ge(wkv_lo, 2)
            for i in range(4):
                sp.dma_start(wqa_raw[:, 2 * i:2 * i + 2, :], wqa_heads[:, 2 * i:2 * i + 2, :])\
                  .then_inc(wqa_loaded[i], 16)
            sp.wait_ge(tr_done, TR_CTX + NT)
            for m in range(MH):
                if m >= 2:
                    sp.wait_ge(fold_done, m - 1)
                sp.dma_start(woa_raw[:, m % 2, :, :, :].rearrange("p o g n -> p o (g n)"),
                             woa_heads[m]).then_inc(woa_loaded[m % 2], 16)
            sp.wait_ge(tr_done, TR_WQA + MH)
            for w, rows in enumerate((wk_rows, wv_rows)):
                sp.dma_start(wkv_raw[:, w, :, :], rows).then_inc(wkv_loaded[w], 16)
            sp.wait_ge(fold_done, MH)
            sp.dma_start(wo_raw, wo_rows[:, 0:GH, :]).then_inc(wo_loaded, 16)
            sp.wait_ge(mm_act, MM_Q1 + MH)
            sp.wait_ge(sig_lo, 2 * MH)
            sp.wait_ge(den_done, 2 * MH)
            for j in range(4):
                if j:
                    sp.wait_ge(wq_lo, j)
                sp.dma_start(wq_raw[:, :, :], wq_rows[:, :, 2 * j * P:(2 * j + 2) * P]).then_inc(wq_loaded, 16)
            for r in range(2):
                sp.wait_ge(kv_written[r], 16 * 16)

            def load_k(g, t):
                sp.dma_start(k_ring[:, t % 4, :, :],
                             keys_dram[bass.ds(g, 1), :, :, t * P:(t + 1) * P].rearrange("g s d n -> d (g s) n"))\
                  .then_inc(k_loaded[t % 4], 16)

            def load_v(g, t):
                for s in range(2):
                    sp.dma_start(v_raw[s * S:(s + 1) * S, t % 2, :, :],
                                 vals_dram[s, t * P:(t + 1) * P, bass.ds(g * P, P)]
                                 .rearrange("(b s) n -> s b n", b=2)).then_inc(v_loaded[t % 2], 16)

            for t in range(3):
                load_k(0, t)
            for t in range(2):
                load_v(0, t)

            def step(g, t, last, first_step=False):
                n = 8 * g + t
                if not (last and t >= 5):
                    if not first_step:
                        sp.wait_ge(scores_done, 2 * n)
                    load_k(g + (t + 3) // 8, (t + 3) % 8)
                if not (last and t >= 6):
                    sp.wait_ge(v_lo, n + 1)
                    load_v(g + (t + 2) // 8, (t + 2) % 8)
                if last:
                    return
                if t == 1:
                    sp.wait_ge(wo_lo, 8 * g + 8)
                    sp.dma_start(wo_raw, wo_rows[:, bass.ds(8 * g + 8, GH), :]).then_inc(wo_loaded, 16)
                if 1 <= t <= 4:
                    j = t - 1
                    sp.wait_ge(wq_lo, 4 * g + 4 + j)
                    sp.dma_start(wq_raw[:, :, :],
                                 wq_rows[:, :, bass.ds((g + 1) * (GH * P) + 2 * j * P, 2 * P)])\
                      .then_inc(wq_loaded, 16)

            step(0, 0, False, True)
            with sp.Fori(0, KV - 1) as g:
                for t in range(1, NT):
                    step(g, t, False)
                step(g + 1, 0, False)
            for t in range(1, NT):
                step(KV - 1, t, True)
                if t == 1:
                    sp.wait_ge(wo_lo, KV * GH)
                    sp.dma_start(rout_rows, router_w).then_inc(expert_loaded, 16)
                    sp.dma_start(rout_b, router_b.rearrange("(a n) -> a n", a=1).broadcast_to([P, NE]))\
                      .then_inc(expert_loaded, 16)
                    sp.dma_start(expert, expert_b).then_inc(expert_loaded, 16)
            for t in range(NT):
                sp.wait_ge(e_out_ready, t + 1)
                sp.dma_start(out_tiles[:, t, :], e_out[:, t % 2, :]).then_inc(out_written[t % 2], 16)
            for r in range(2):
                sp.wait_ge(out_written[r], 16 * NT // 2)

        @block.gpsimd
        def _(pool):
            nc.gpsimd.memset(neg_half[:, :], -0.5).then_inc(consts_set, 1)
            nc.gpsimd.memset(ident[:, :], 0.0).then_inc(consts_set, 1)
            pool.wait_ge(consts_set, 2)
            nc.gpsimd.affine_select(out=ident[:, :], in_=ident[:, :], compare_op=ALU.not_equal, fill=1.0,
                                    base=0, pattern=[[-1, P]], channel_multiplier=1).then_inc(consts_set, 1)

            def root(k):
                pool.wait_ge(var_ready, k + 1)
                nc.gpsimd.tensor_tensor(rstd[:, :], vareps[:, :], neg_half[:, :], ALU.pow)\
                    .then_inc(rstd_ready, 1)

            for t in range(NT):
                root(t)
            for m in range(MH):
                pool.wait_ge(woa_loaded[m % 2], 16 * (m // 2 + 1))
                w = woa_raw[:, m % 2, :, :, :]
                nc.gpsimd.tensor_tensor(w[:, :, 0:2, :], w[:, :, 0:2, :], w[:, :, 2:4, :], ALU.add)\
                    .then_inc(fold_half, 1)
                pool.wait_ge(fold_half, m + 1)
                if m >= 2:
                    pool.wait_ge(tr_done, TR_MEM + 2 * (m - 2) + 2)
                nc.gpsimd.tensor_tensor(wofold[:, m % 2, :, :], w[:, :, 0, :], w[:, :, 1, :], ALU.add)\
                    .then_inc(fold_done, 1)
            for k in range(NT, 3 * NT):
                root(k)

        @block.tensor
        def _(pe):
            pe.wait_ge(consts_set, 3)

            def tr_free(k):
                if k >= 2:
                    pe.wait_ge(tr_used, k - 1)

            def mm_free(k):
                if k >= 2:
                    pe.wait_ge(mm_act, k - 1)
                    if mm_dve_count(k - 2):
                        pe.wait_ge(mm_dve, mm_dve_count(k - 2))

            def transpose_rows(k, rows):
                tr_free(k)
                for c in range(KC):
                    last = nc.tensor.transpose(tr_bank(k)[:, c * P:(c + 1) * P],
                                               rows[:, c * P:(c + 1) * P], ident[:, :])
                last.then_inc(tr_done, 1)

            def product(k, left, right):
                mm_free(k)
                terms = [(a, b, c) for c in range(KC) for a, b in PARTS]
                for i, (a, b, c) in enumerate(terms):
                    last = nc.tensor.matmul(mm_bank(k)[:, :], left(a, c), right(b, c),
                                            start=i == 0, stop=i == len(terms) - 1)
                last.then_inc(mm_done, 1)

            for t in range(NT):
                if t % 2 == 0:
                    pe.wait_ge(ctx_loaded[t // 2], 16)
                transpose_rows(TR_CTX + t, ctx_raw[:, t, :])

            def keys(base, wkv, srcT):
                for g in range(KV):
                    for half in range(2):
                        product(base + 2 * g + half,
                                lambda a, c: wkv[:, a, 0, c, g * P:(g + 1) * P],
                                lambda b, c: srcT[:, b, c, half * HALF:(half + 1) * HALF])

            def values(k, wkv, srcT, t):
                product(k, lambda a, c: srcT[:, a, c, t * P:(t + 1) * P],
                        lambda b, c: wkv[:, b, 1, c, :])

            pe.wait_ge(tr_used, TR_CTX + NT)
            pe.wait_ge(wkv_lo, 1)
            keys(MM_KCTX, wkv1, ctxT)
            pe.wait_ge(wkv_lo, 2)
            for t in range(NT):
                values(MM_VCTX + t, wkv1, ctxT, t)
                pe.wait_ge(xn_ready, t + 1)
                transpose_rows(TR_X + t, xn[:, t % 2, :])

            pe.wait_ge(bz_loaded, 32)
            tr_free(TR_BZ)
            nc.tensor.transpose(tr_bank(TR_BZ)[:, 0:2 * MH], bz_rows, ident[0:2 * MH, 0:2 * MH])\
                .then_inc(tr_done, 1)

            def memory_wq(m):
                if m % 2 == 0:
                    pe.wait_ge(wqa_loaded[m // 2], 16)
                transpose_rows(TR_WQA + m, wqa_raw[:, m, :])

            def denominators(half, m):
                pe.wait_ge(sig_ready, half * MH + m + 1)
                for i in range(4):
                    col = (half * 4 + i) * MH + m
                    last = nc.tensor.matmul(den_bank[:, col:col + 1], sig[:, m % 2, i * P:(i + 1) * P],
                                            bz[:, MH + m:MH + m + 1], start=True, stop=True)
                last.then_inc(den_done, 1)

            def memory_queries(half):
                for m in range(MH):
                    if half == 0:
                        pe.wait_ge(tr_used, TR_WQA + m + 1)
                    product((MM_Q0, MM_Q1)[half] + m,
                            lambda a, c: wqaT[:, a, m, c, :],
                            lambda b, c: xnT[:, b, c, half * HALF:(half + 1) * HALF])
                    if half == 0 and m + 2 < MH:
                        memory_wq(m + 2)
                    if m >= 1:
                        denominators(half, m - 1)
                denominators(half, MH - 1)

            memory_wq(0)
            memory_wq(1)
            memory_queries(0)
            def memory_transposes(m):
                k = TR_MEM + 2 * m
                if m == 0:
                    pe.wait_ge(mem_loaded, 16)
                tr_free(k)
                nc.tensor.transpose(tr_bank(k)[:, 0:P], mem[:, m, :], ident[:, :]).then_inc(tr_done, 1)
                pe.wait_ge(fold_done, m + 1)
                tr_free(k + 1)
                for c in range(KC):
                    last = nc.tensor.transpose(tr_bank(k + 1)[:, c * P:(c + 1) * P],
                                               wofold[:, m % 2, c, :], ident[:, :])
                last.then_inc(tr_done, 1)

            for m in range(MH):
                memory_transposes(m)
                k = MM_MW + m
                mm_free(k)
                pe.wait_ge(tr_used, TR_MEM + 2 * m + 2)
                for i, (a, b) in enumerate(PARTS):
                    last = nc.tensor.matmul(mm_bank(k)[:, :], memT[:, a, :], wofT[:, b, :],
                                            start=i == 0, stop=i == 2)
                last.then_inc(mm_done, 1)

            def memory_output(half):
                for t in range(4 * half, 4 * half + 4):
                    for m in range(MH):
                        k = MH * t + m
                        if k >= 3:
                            pe.wait_ge(y_used, k - 2)
                        if t % 4 == 0:
                            pe.wait_ge(sig_lo, half * MH + m + 1)
                        if t == 0:
                            pe.wait_ge(mm_dve, mm_dve_count(MM_MW + m))
                        for i, (a, b) in enumerate(PARTS):
                            last = nc.tensor.matmul(y_bank(k)[:, :],
                                                    sigT[:, a, m, (t % 4) * P:(t % 4 + 1) * P],
                                                    memwo[:, b, m, :], start=i == 0, stop=i == 2)
                        last.then_inc(y_done, 1)
                    if t >= 1 and t != 4:
                        latent_transposes(t - 1)

            def latent_transposes(t):
                pe.wait_ge(xn_ready, NT + t + 1)
                transpose_rows(TR_X2 + t, xn[:, t % 2, :])

            memory_output(0)
            memory_queries(1)
            latent_transposes(3)
            memory_output(1)
            pe.wait_ge(wkv_lo, 4)
            for t in range(4):
                values(MM_VLAT + t, wkv2, xnT, t)
            latent_transposes(7)
            for t in range(4, NT):
                pe.wait_ge(tr_used, TR_X2 + t + 1)
                values(MM_VLAT + t, wkv2, xnT, t)
            keys(MM_KLAT, wkv2, xnT)

            def queries(k_bank, head, half, done):
                for i, (c, (a, b)) in enumerate((c, ab) for c in range(KC) for ab in PARTS):
                    last = nc.tensor.matmul(k_bank[:, :], wq[:, a, head, c, :],
                                            xnT[:, b, c, half * HALF:(half + 1) * HALF],
                                            start=i == 0, stop=i == 3 * KC - 1)
                last.then_inc(done, 1)

            for h in range(GH):
                k = MM_XQ + h
                mm_free(k)
                if h % 2 == 0:
                    pe.wait_ge(wq_lo, h // 2 + 1)
                queries(mm_bank(k), h, 0, mm_done)

            def project(g, t, parity, release):
                n = 8 * g + t
                pe.wait_ge(oT_lo, 2 * n + 2)
                pe.wait_ge(proj_added, n + 1)
                for h in range(GH):
                    if t == 0:
                        pe.wait_ge(wo_lo, 8 * g + h + 1)
                    for i, (a, b) in enumerate(PARTS):
                        last = nc.tensor.matmul(bank[7][:, :], oT[:, parity, a, h, :], wo[:, b, h, :],
                                                start=h == 0 and i == 0, stop=h == GH - 1 and i == 2)
                    if release and h < GH - 1:
                        last.then_inc(wo_used, 1)
                last.then_inc(proj_done, 1)

            def step(g, t, last_group, first_step=False):
                n = 8 * g + t
                half = t // 4
                if first_step:
                    pe.wait_ge(mm_act, MM_XQ + GH)
                    pe.wait_ge(tr_used, TR_X2 + NT)
                elif t % 4 == 0:
                    pe.wait_ge(q_saved, 16 * g + 2 * t)
                pe.wait_ge(k_loaded[t % 4], 16 * (2 * g + half + 1))
                for bb in range(2):
                    if not first_step:
                        pe.wait_ge(exp_done, 2 * n - 1 + bb)
                    for p in range(4):
                        last = nc.tensor.matmul(bank[bb][:, p * P:(p + 1) * P],
                                                qT[:, half, (2 * t + bb) % 8, 2 * p:2 * p + 2, :]
                                                .rearrange("p h s -> p (h s)"),
                                                k_ring[:, t % 4, :, bb * S:(bb + 1) * S],
                                                start=True, stop=True)
                    last.then_inc(scores_done, 1)

                def next_queries(u):
                    if last_group and t >= 4:
                        return
                    k = 16 * g + 2 * t + u
                    if first_step and u == 0:
                        pe.wait_ge(y_used, MH * NT)
                    else:
                        pe.wait_ge(q_saved, k)
                    head = 2 * (t % 4) + u
                    if t >= 4 and u == 0:
                        pe.wait_ge(wq_lo, 4 * g + 4 + t - 3)
                    queries(bank[6], head, 1 - half, q_done)

                next_queries(0)
                if not first_step:
                    if t == 0:
                        project(g - 1, 7, 1, True)
                    else:
                        project(g, t - 1, (t - 1) % 2, False)
                for bb in range(2):
                    pe.wait_ge(probs_ready, 2 * n + bb + 1)
                    if not first_step:
                        pe.wait_ge(pT_lo, 2 * n - 1 + bb)
                    for p in range(4):
                        last = nc.tensor.transpose(bank[2 + bb][:, p * P:(p + 1) * P],
                                                   probs[:, bb, p, :], ident[:, :])
                    last.then_inc(pT_done, 1)
                next_queries(1)
                pe.wait_ge(v_lo, n + 1)
                for bb in range(2):
                    pe.wait_ge(pT_lo, 2 * n + bb + 1)
                    if first_step:
                        pe.wait_ge(rden_ready, 2)
                    else:
                        pe.wait_ge(oT_lo, 2 * n - 1 + bb)
                    for i, (a, b) in enumerate(PARTS):
                        last = nc.tensor.matmul(bank[4 + bb][:, :], v_ring[:, t % 2, bb, a, :],
                                                pT[:, bb, b, :], start=i == 0, stop=i == 2)
                    last.then_inc(pv_done, 1)

            step(0, 0, False, True)
            with pe.Fori(0, KV - 1) as g:
                for t in range(1, NT):
                    step(g, t, False)
                step(g + 1, 0, False)
            for t in range(1, NT):
                step(KV - 1, t, True)
            project(KV - 1, NT - 1, 1, False)

            pe.wait_ge(expert_loaded, 48)
            pe.wait_ge(oT_lo, 2 * KV * NT)
            for c in range(KC):
                last = nc.tensor.transpose(bank[4][:, c * NE:(c + 1) * NE],
                                           rout_rows[:, c * P:(c + 1) * P], ident[0:NE, 0:NE])
            last.then_inc(routT_done, 1)
            for t in range(NT):
                pe.wait_ge(e_xn_ready, t + 1)
                if t >= 2:
                    pe.wait_ge(e_xnT_ready, t - 1)
                for c in range(KC):
                    last = nc.tensor.transpose(bank[t % 2][:, c * P:(c + 1) * P],
                                               e_xn[:, t % 2, c * P:(c + 1) * P], ident[:, :])
                last.then_inc(e_tr_done, 1)
                pe.wait_ge(e_xnT_ready, t + 1)
                if t == 0:
                    pe.wait_ge(routT_ready, 1)
                if t >= 2:
                    pe.wait_ge(logits_saved, t - 1)
                for c in range(KC):
                    last = nc.tensor.matmul(bank[2 + t % 2][:, 0:NE], e_xnT[:, t % 2, c, :], routT[:, c, :],
                                            start=c == 0, stop=c == KC - 1)
                last.then_inc(logits_done, 1)
                pe.wait_ge(e_w_ready, t + 1)
                if t >= 2:
                    pe.wait_ge(e_wT_ready, t - 1)
                nc.tensor.transpose(bank[4 + t % 2][0:NE, 0:P], small[:, t % 2, 4, :], ident[:, :])\
                    .then_inc(e_wT_done, 1)
                pe.wait_ge(e_wT_ready, t + 1)
                if t >= 2:
                    pe.wait_ge(e_out_ready, t - 1)
                nc.tensor.matmul(bank[6 + t % 2][:, :], e_wT[:, t % 2, :], expert[:, :], start=True, stop=True)\
                    .then_inc(mix_done, 1)

        @block.scalar
        def _(act):
            def high(dst, src):
                return nc.scalar.copy(dst, src)

            def wq_high(g, j):
                act.wait_ge(wq_loaded, 16 * (4 * g + j + 1))
                high(wq[:, 0, 2 * j:2 * j + 2, :, :],
                     wq_raw[:, :, :].rearrange("p k (h n) -> p h k n", h=2)).then_inc(wq_hi, 1)

            def v_high(g, t):
                act.wait_ge(v_loaded[t % 2], 32 * (4 * g + t // 2 + 1))
                high(v_ring[:, t % 2, :, 0, :], v_raw[:, t % 2, :, :]).then_inc(v_hi, 1)

            def wo_high(g, h):
                high(wo[:, 0, h, :], wo_raw[:, h, :]).then_inc(wo_hi, 1)

            def save_queries(k_bank, half, head, saved):
                nc.scalar.mul(qT[:, half, :, head, :], k_bank[:, :].rearrange("p (b s) -> p b s", b=8), SCALE)\
                    .then_inc(saved, 1)

            def tr_high(k, dst, src=None):
                act.wait_ge(tr_done, k + 1)
                high(dst, tr_bank(k)[:, :] if src is None else src).then_inc(tr_hi, 1)

            def blocks(k):
                return tr_bank(k)[:, :].rearrange("p (c n) -> p c n", c=KC)

            for t in range(NT):
                tr_high(TR_CTX + t, ctxT[:, 0, :, t * P:(t + 1) * P], blocks(TR_CTX + t))
            for w in range(2):
                act.wait_ge(wkv_loaded[w], 16)
                high(wkv1[:, 0, w, :, :], wkv_raw[:, w, :, :]).then_inc(wkv_hi, 1)

            def save_kv(k, n, dst):
                act.wait_ge(mm_done, k + 1)
                if n >= 2:
                    act.wait_ge(kv_written[n % 2], 16 * (n // 2))
                nc.scalar.copy(kvout[:, n % 2, :], mm_bank(k)[:, :]).then_inc(mm_act, 1)
                act.wait_ge(mm_act, k + 1)
                act.dma_start(dst, kvout[:, n % 2, :]).then_inc(kv_written[n % 2], 16)

            def save_keys(base, n, s):
                for g in range(KV):
                    for half in range(2):
                        i = 2 * g + half
                        save_kv(base + i, n + i, keys_dram[g, s, :, half * HALF:(half + 1) * HALF])

            save_keys(MM_KCTX, 0, 0)
            for t in range(NT):
                save_kv(MM_VCTX + t, 8 + t, vals_dram[0, t * P:(t + 1) * P, :])
                tr_high(TR_X + t, xnT[:, 0, :, t * P:(t + 1) * P], blocks(TR_X + t))

            def memory_wq(m):
                tr_high(TR_WQA + m, wqaT[:, 0, m, :, :], blocks(TR_WQA + m))

            def memory_queries(half):
                for m in range(MH):
                    k = (MM_Q0, MM_Q1)[half] + m
                    i = half * MH + m
                    if i == 0:
                        act.wait_ge(tr_used, TR_BZ + 1)
                    act.wait_ge(mm_dve, mm_dve_count(k))
                    if i:
                        act.wait_ge(sig_ready, i)
                    nc.scalar.activation(qpos[:, :], mm_bank(k)[:, :], ACT.Relu, bias=bz[:, m:m + 1])\
                        .then_inc(mm_act, 1)
                    nc.scalar.activation(qneg[:, :], qneg[:, :], ACT.Exp).then_inc(qexp_ready, 1)
                    act.wait_ge(sig_ready, i + 1)
                    high(sigT[:, 0, m, :], sig[:, i % 2, :]).then_inc(sig_hi, 1)
                    if half == 0 and m + 2 < MH:
                        memory_wq(m + 2)

            memory_wq(0)
            memory_wq(1)
            memory_queries(0)
            for m in range(MH):
                k = TR_MEM + 2 * m
                if m:
                    act.wait_ge(mm_done, MM_MW + m)
                tr_high(k, memT[:, 0, :], tr_bank(k)[:, 0:P])
                tr_high(k + 1, wofT[:, 0, :])
                act.wait_ge(mm_done, MM_MW + m + 1)
                high(memwo[:, 0, m, :], mm_bank(MM_MW + m)[:, :]).then_inc(mm_act, 1)

            def latent_high(t):
                tr_high(TR_X2 + t, xnT[:, 0, :, t * P:(t + 1) * P], blocks(TR_X2 + t))

            for t in range(3):
                latent_high(t)
            act.wait_ge(y_done, MH * 4)
            memory_queries(1)
            for w in range(2):
                act.wait_ge(wkv_loaded[w], 32)
                high(wkv2[:, 0, w, :, :], wkv_raw[:, w, :, :]).then_inc(wkv_hi, 1)
            for t in range(3, 7):
                latent_high(t)
            for t in range(4):
                save_kv(MM_VLAT + t, 16 + t, vals_dram[1, t * P:(t + 1) * P, :])
            latent_high(7)
            for t in range(4, NT):
                save_kv(MM_VLAT + t, 16 + t, vals_dram[1, t * P:(t + 1) * P, :])
                if t == 4:
                    act.wait_ge(y_done, MH * NT)
                wq_high(0, t - 4)
            save_keys(MM_KLAT, 24, 1)
            v_high(0, 0)
            for h in range(GH):
                k = MM_XQ + h
                act.wait_ge(mm_done, k + 1)
                save_queries(mm_bank(k), 0, h, mm_act)
                if h == 0:
                    act.wait_ge(wo_loaded, 16)
                wo_high(0, h)

            def step(g, t, last_group, first_step=False):
                n = 8 * g + t
                half = t // 4
                for bb in range(2):
                    act.wait_ge(negmax_ready, 2 * n + bb + 1)
                    if not first_step:
                        act.wait_ge(pT_done, 2 * n - 1 + bb)
                    for p in range(4):
                        last = nc.scalar.activation(probs[:, bb, p, :], bank[bb][:, p * P:(p + 1) * P], ACT.Exp,
                                                    bias=negmax[:, bb, p:p + 1],
                                                    accum_out=rowsum[:, bb, p:p + 1])
                    last.then_inc(exp_done, 1)

                def save_next(u):
                    if last_group and t >= 4:
                        return
                    act.wait_ge(q_done, 16 * g + 2 * t + u + 1)
                    save_queries(bank[6], 1 - half, 2 * (t % 4) + u, q_saved)

                save_next(0)
                if not (last_group and t == 7):
                    if not first_step:
                        act.wait_ge(pv_done, 2 * n)
                    v_high(g, t + 1)
                if not last_group and 2 <= t <= 5:
                    act.wait_ge(q_done, 16 * g + 2 * (t - 2) + 2)
                    wq_high(g + 1, t - 2)
                if t == 0 and not first_step:
                    act.wait_ge(wo_loaded, 16 * g + 16)
                    for h in range(GH):
                        if h < GH - 1:
                            act.wait_ge(wo_used, (GH - 1) * (g - 1) + h + 1)
                        else:
                            act.wait_ge(proj_done, 8 * g)
                        wo_high(g, h)
                for bb in range(2):
                    act.wait_ge(pT_done, 2 * n + bb + 1)
                    if not first_step:
                        act.wait_ge(pv_done, 2 * n - 1 + bb)
                    high(pT[:, bb, 0, :], bank[2 + bb][:, :]).then_inc(pT_hi, 1)
                save_next(1)
                for bb in range(2):
                    act.wait_ge(pv_done, 2 * n + bb + 1)
                    high(oT[:, t % 2, 0, :, bb * S:(bb + 1) * S],
                         bank[4 + bb][:, :].rearrange("p (h s) -> p h s", h=GH)).then_inc(oT_hi, 1)

            step(0, 0, False, True)
            with act.Fori(0, KV - 1) as g:
                for t in range(1, NT):
                    step(g, t, False)
                step(g + 1, 0, False)
            for t in range(1, NT):
                step(KV - 1, t, True)

            for t in range(NT):
                act.wait_ge(e_tr_done, t + 1)
                if t >= 2:
                    act.wait_ge(logits_done, t - 1)
                nc.scalar.copy(e_xnT[:, t % 2, :, :], bank[t % 2][:, :].rearrange("p (k n) -> p k n", k=KC))\
                    .then_inc(e_xnT_ready, 1)
                act.wait_ge(e_max_ready, t + 1)
                nc.scalar.activation(small[:, t % 2, 1, :], small[:, t % 2, 0, :], ACT.Exp,
                                     bias=top[:, t % 2, 1, 0:1], accum_out=top[:, t % 2, 2, 0:1])\
                    .then_inc(e_exp_done, 1)
                act.wait_ge(e_wT_done, t + 1)
                if t >= 2:
                    act.wait_ge(mix_done, t - 1)
                nc.scalar.copy(e_wT[:, t % 2, :], bank[4 + t % 2][0:NE, 0:P]).then_inc(e_wT_ready, 1)

        @block.vector
        def _(dve):
            steps = [0]

            def settled(ins):
                steps[0] += 1
                ins.then_inc(dve_step, 1)
                dve.wait_ge(dve_step, steps[0])

            def low(dst, src, high):
                return nc.vector.tensor_tensor(dst, src, high.bitcast(F), ALU.subtract)

            def blocks(k):
                return tr_bank(k)[:, :].rearrange("p (c n) -> p c n", c=KC)

            def tr_low(k, dst, src, high):
                dve.wait_ge(tr_hi, tr_hi_count(k))
                low(dst, src, high).then_inc(tr_used, 1)

            def normalise(k, src, dst, done):
                settled(nc.vector.bn_stats(stats[:, :], src))
                settled(nc.vector.bn_aggr(meanvar[:, :], stats[:, :]))
                nc.vector.tensor_scalar(vareps[:, :], meanvar[:, 1:2], LN_EPS, None, ALU.add)\
                    .then_inc(var_ready, 1)
                dve.wait_ge(rstd_ready, k + 1)
                nc.vector.tensor_scalar(dst, src, meanvar[:, 0:1], rstd[:, 0:1],
                                        ALU.subtract, ALU.mult).then_inc(done, 1)

            for t in range(NT):
                cols = slice(t * P, (t + 1) * P)
                tr_low(TR_CTX + t, ctxT[:, 1, :, cols], blocks(TR_CTX + t), ctxT[:, 0, :, cols])
            for w in range(2):
                dve.wait_ge(wkv_hi, w + 1)
                low(wkv1[:, 1, w, :, :], wkv_raw[:, w, :, :], wkv1[:, 0, w, :, :]).then_inc(wkv_lo, 1)

            def norm_x(t):
                if t % 2 == 0:
                    dve.wait_ge(x_loaded[t // 2], 16)
                if t >= 2:
                    dve.wait_ge(tr_done, TR_X + t - 1)
                normalise(t, resid[:, t, :], xn[:, t % 2, :], xn_ready)

            def x_low(base, t):
                cols = slice(t * P, (t + 1) * P)
                tr_low(base + t, xnT[:, 1, :, cols], blocks(base + t), xnT[:, 0, :, cols])

            norm_x(0)
            for t in range(NT):
                if t + 1 < NT:
                    norm_x(t + 1)
                x_low(TR_X, t)
            dve.wait_ge(tr_done, TR_BZ + 1)
            nc.vector.tensor_copy(bz[:, :], tr_bank(TR_BZ)[:, 0:2 * MH]).then_inc(tr_used, 1)
            dve.wait_ge(tr_used, TR_BZ + 1)

            def memory_wq(m):
                tr_low(TR_WQA + m, wqaT[:, 1, m, :, :], blocks(TR_WQA + m), wqaT[:, 0, m, :, :])

            def reciprocal_denominators(half):
                dve.wait_ge(den_done, MH * (half + 1))
                r = rden[:, half, :, :].rearrange("p t m -> p (t m)")
                settled(nc.vector.tensor_scalar(r, den_bank[:, half * 4 * MH:(half + 1) * 4 * MH],
                                                DEN_EPS, None, ALU.add))
                nc.vector.reciprocal(r, r).then_inc(rden_ready, 1)

            def memory_queries(half):
                for m in range(MH):
                    k = (MM_Q0, MM_Q1)[half] + m
                    i = half * MH + m
                    dve.wait_ge(mm_done, k + 1)
                    nc.vector.tensor_scalar(qneg[:, :], mm_bank(k)[:, :], bz[:, m:m + 1], 0.0,
                                            ALU.add, ALU.min)\
                        .then_inc(mm_dve, 1)
                    if i >= 2:
                        dve.wait_ge(den_done, i - 1)
                        dve.wait_ge(sig_hi, i - 1)
                    dve.wait_ge(qexp_ready, i + 1)
                    nc.vector.tensor_tensor(sig[:, i % 2, :], qneg[:, :], qpos[:, :], ALU.add)\
                        .then_inc(sig_ready, 1)
                    dve.wait_ge(sig_hi, i + 1)
                    low(sigT[:, 1, m, :], sig[:, i % 2, :], sigT[:, 0, m, :]).then_inc(sig_lo, 1)
                    if half == 0 and m + 2 < MH:
                        memory_wq(m + 2)
                reciprocal_denominators(half)

            memory_wq(0)
            memory_wq(1)
            memory_queries(0)
            for m in range(MH):
                k = TR_MEM + 2 * m
                tr_low(k, memT[:, 1, :], tr_bank(k)[:, 0:P], memT[:, 0, :])
                tr_low(k + 1, wofT[:, 1, :], tr_bank(k + 1)[:, :], wofT[:, 0, :])
                dve.wait_ge(mm_act, MM_MW + m + 1)
                low(memwo[:, 1, m, :], mm_bank(MM_MW + m)[:, :], memwo[:, 0, m, :]).then_inc(mm_dve, 1)

            def add_memory(t):
                if t % 4 == 0:
                    dve.wait_ge(rden_ready, t // 4 + 1)
                for m in range(MH):
                    k = MH * t + m
                    dve.wait_ge(y_done, k + 1)
                    if m:
                        dve.wait_ge(y_used, k)
                    last = nc.vector.scalar_tensor_tensor(out=resid[:, t, :], in0=y_bank(k)[:, :],
                                                          scalar=rden[:, t // 4, t % 4, m:m + 1],
                                                          in1=resid[:, t, :], op0=ALU.mult, op1=ALU.add)
                    last.then_inc(y_used, 1)
                dve.wait_ge(y_used, MH * t + MH)
                if t >= 2:
                    dve.wait_ge(tr_done, TR_X2 + t - 1)
                normalise(NT + t, resid[:, t, :], xn[:, t % 2, :], xn_ready)

            for t in range(4):
                add_memory(t)
                if t:
                    x_low(TR_X2, t - 1)
            memory_queries(1)
            for w in range(2):
                dve.wait_ge(wkv_hi, w + 3)
                low(wkv2[:, 1, w, :, :], wkv_raw[:, w, :, :], wkv2[:, 0, w, :, :]).then_inc(wkv_lo, 1)
            x_low(TR_X2, 3)
            for t in range(4, NT):
                add_memory(t)
                if t > 4:
                    x_low(TR_X2, t - 1)
            x_low(TR_X2, 7)

            def wq_low(g, j):
                dve.wait_ge(wq_hi, 4 * g + j + 1)
                low(wq[:, 1, 2 * j:2 * j + 2, :, :], wq_raw[:, :, :].rearrange("p k (h n) -> p h k n", h=2),
                    wq[:, 0, 2 * j:2 * j + 2, :, :]).then_inc(wq_lo, 1)

            def v_low(g, t):
                dve.wait_ge(v_hi, 8 * g + t + 1)
                low(v_ring[:, t % 2, :, 1, :], v_raw[:, t % 2, :, :], v_ring[:, t % 2, :, 0, :]).then_inc(v_lo, 1)

            def wo_low(g, h):
                dve.wait_ge(wo_hi, 8 * g + h + 1)
                low(wo[:, 1, h, :], wo_raw[:, h, :], wo[:, 0, h, :]).then_inc(wo_lo, 1)

            for j in range(4):
                wq_low(0, j)
            v_low(0, 0)
            for h in range(GH):
                wo_low(0, h)
            nc.vector.tensor_copy(stats[:, 0:1], meanvar[:, 0:1]).then_inc(proj_added, 1)

            def step(g, t, last_group, first_step=False):
                n = 8 * g + t
                for bb in range(2):
                    dve.wait_ge(scores_done, 2 * n + bb + 1)
                    nc.vector.tensor_reduce(negmax[:, bb, :], bank[bb][:, :].rearrange("p (c n) -> p c n", c=4),
                                            axis=AX, op=ALU.max, negate=True).then_inc(negmax_ready, 1)
                for bb in range(2):
                    dve.wait_ge(exp_done, 2 * n + bb + 1)
                    nc.vector.reciprocal(rrow[:, bb, :], rowsum[:, bb, :]).then_inc(rrow_ready, 1)
                    dve.wait_ge(rrow_ready, 2 * n + bb + 1)
                    nc.vector.tensor_tensor(probs[:, bb, :, :], probs[:, bb, :, :],
                                            rrow[:, bb, :].unsqueeze(2).broadcast_to([P, 4, P]),
                                            ALU.mult).then_inc(probs_ready, 1)
                if not (last_group and t == 7):
                    v_low(g, t + 1)
                if not last_group and 2 <= t <= 5:
                    wq_low(g + 1, t - 2)
                if t == 0 and not first_step:
                    for h in range(GH):
                        wo_low(g, h)
                if not first_step:
                    dve.wait_ge(proj_done, n)
                    rows = resid[:, (t - 1) % NT, :]
                    nc.vector.tensor_tensor(rows, rows, bank[7][:, :], ALU.add).then_inc(proj_added, 1)
                for bb in range(2):
                    dve.wait_ge(pT_hi, 2 * n + bb + 1)
                    low(pT[:, bb, 1, :], bank[2 + bb][:, :], pT[:, bb, 0, :]).then_inc(pT_lo, 1)
                for bb in range(2):
                    dve.wait_ge(oT_hi, 2 * n + bb + 1)
                    cols = slice(bb * S, (bb + 1) * S)
                    low(oT[:, t % 2, 1, :, cols], bank[4 + bb][:, :].rearrange("p (h s) -> p h s", h=GH),
                        oT[:, t % 2, 0, :, cols]).then_inc(oT_lo, 1)

            step(0, 0, False, True)
            with dve.Fori(0, KV - 1) as g:
                for t in range(1, NT):
                    step(g, t, False)
                step(g + 1, 0, False)
            for t in range(1, NT):
                step(KV - 1, t, True)
            dve.wait_ge(proj_done, KV * NT)
            settled(nc.vector.tensor_tensor(resid[:, 7, :], resid[:, 7, :], bank[7][:, :], ALU.add))

            dve.wait_ge(routT_done, 1)
            nc.vector.tensor_copy(routT, bank[4][:, 0:KC * NE].rearrange("p (k n) -> p k n", k=KC))\
                .then_inc(routT_ready, 1)
            for t in range(NT):
                r = t % 2
                if t >= 2:
                    dve.wait_ge(e_tr_done, t - 1)
                normalise(2 * NT + t, resid[:, t, :], e_xn[:, r, :], e_xn_ready)
                logits, expd, score, rest, weight = (small[:, r, i, :] for i in range(5))
                dve.wait_ge(logits_done, t + 1)
                nc.vector.tensor_tensor(logits, bank[2 + r][:, 0:NE], rout_b, ALU.add).then_inc(logits_saved, 1)
                dve.wait_ge(logits_saved, t + 1)
                settled(nc.vector.max(top[:, r, 0, :], logits))
                nc.vector.tensor_scalar(top[:, r, 1, 0:1], top[:, r, 0, 0:1], -1.0, None, ALU.mult)\
                    .then_inc(e_max_ready, 1)
                dve.wait_ge(e_exp_done, t + 1)
                settled(nc.vector.reciprocal(top[:, r, 2, 1:2], top[:, r, 2, 0:1]))
                settled(nc.vector.tensor_scalar(score, expd, top[:, r, 2, 1:2], None, ALU.mult))
                settled(nc.vector.max(top[:, r, 3, :], score))
                nc.vector.tensor_reduce(top[:, r, 2, 2:3], top[:, r, 3, :], axis=AX, op=ALU.add)
                settled(nc.vector.match_replace(rest, top[:, r, 3, :], score, 0.0))
                if t >= 2:
                    dve.wait_ge(e_wT_done, t - 1)
                nc.vector.tensor_tensor(weight, score, rest, ALU.subtract).then_inc(e_w_ready, 1)
                if t >= 2:
                    dve.wait_ge(out_written[r], 16 * (t // 2))
                if t == 1:
                    dve.wait_ge(routT_ready, 1)
                settled(nc.vector.scalar_tensor_tensor(out=e_out[:, r, :], in0=e_xn[:, r, :],
                                                       scalar=top[:, r, 2, 2:3], in1=resid[:, t, :],
                                                       op0=ALU.mult, op1=ALU.add))
                dve.wait_ge(mix_done, t + 1)
                nc.vector.tensor_tensor(e_out[:, r, :], e_out[:, r, :], bank[6 + r][:, :], ALU.add)\
                    .then_inc(e_out_ready, 1)


_INS = ["x", "ctx_4096", "L0_attn_Wq", "L0_attn_bq", "L0_attn_Wo", "L0_attn_M", "L0_attn_z",
        "L0_xattn_Wq", "L0_xattn_Wk", "L0_xattn_Wv", "L0_xattn_Wo",
        "L0_ffn_router_weight", "L0_ffn_router_bias", "L0_ffn_expert_bias"]


def kernel(**inputs):
    import numpy as _np
    import concourse.bacc as _bacc
    from concourse import mybir as _mybir
    from concourse.bass_utils import run_bass_kernel_spmd as _run

    nc = _bacc.Bacc("TRN2", target_bir_lowering=False, num_devices=1)
    arrays, args = {}, []
    for name in _INS:
        a = _np.ascontiguousarray(inputs[name])
        arrays[f"in_{name}"] = a
        args.append(nc.dram_tensor(f"in_{name}", a.shape, _mybir.dt.from_np(a.dtype), kind="ExternalInput").ap())
    shape = inputs["x"].shape
    args.append(nc.dram_tensor("out_x", shape, _mybir.dt.float32, kind="ExternalOutput").ap())
    decoder_layer(nc, *args)
    r = _run(nc, [arrays], core_ids=[0])
    return r.results[0]["out_x"]
```

```python
import concourse.bass as bass
import numpy as np
from concourse import mybir
from contextlib import ExitStack


def decoder_layer(
    nc: bass.Bass,
    x_in: bass.AP,
    ctx_in: bass.AP,
    attn_Wq: bass.AP,
    attn_bq: bass.AP,
    attn_Wo: bass.AP,
    attn_M: bass.AP,
    attn_z: bass.AP,
    x_Wq: bass.AP,
    x_Wk: bass.AP,
    x_Wv: bass.AP,
    x_Wo: bass.AP,
    router_w: bass.AP,
    router_b: bass.AP,
    expert_b: bass.AP,
    out: bass.AP,
):
    F = mybir.dt.float32
    R = mybir.dt.float32r
    ALU = mybir.AluOpType
    ACT = mybir.ActivationFunctionType
    AX = mybir.AxisListType.X

    P = 128
    B, S, D = x_in.shape
    NT = B * S // P
    KC = D // P
    NTOK = B * S
    HALF = NTOK // 2
    H = attn_Wq.shape[0] // P
    MH = attn_M.shape[0]
    GREP = H // MH
    KV = x_Wk.shape[1] // P
    GH = H // KV
    NE = router_w.shape[0]
    SCALE = float(P) ** -0.5
    LN_EPS = 1e-5
    DEN_EPS = 1e-6
    assert (NT, KC, H, MH, KV, GH, NE) == (8, 4, 32, 8, 4, 8, 64)

    x_tiles = x_in.rearrange("b s d -> (b s) d").rearrange("(t p) d -> p t d", p=P)
    ctx_tiles = ctx_in.rearrange("b s d -> (b s) d").rearrange("(t p) d -> p t d", p=P)
    out_tiles = out.rearrange("b s d -> (b s) d").rearrange("(t p) d -> p t d", p=P)
    wqa_heads = attn_Wq.rearrange("(m g p) k -> g p m k", g=GREP, p=P)[0]
    bq_rows = attn_bq.rearrange("(m g p) -> g m p", g=GREP, p=P)[0]
    woa_heads = attn_Wo.rearrange("(o p) (m c) -> m p o c", p=P, m=MH)
    mem_heads = attn_M.rearrange("m d e -> d m e")
    wk_rows = x_Wk.rearrange("(k p) n -> p k n", p=P)
    wv_rows = x_Wv.rearrange("(k p) n -> p k n", p=P)
    wq_rows = x_Wq.rearrange("(k p) n -> p k n", p=P)
    wo_rows = x_Wo.rearrange("(h p) n -> p h n", p=P)

    keys_dram = nc.dram_tensor("keys_dram", (KV, 2, P, NTOK), F, kind="Internal").ap()
    vals_dram = nc.dram_tensor("vals_dram", (2, NTOK, KV * P), F, kind="Internal").ap()

    ctx = ExitStack()
    with ctx:
        def sb(name, shape, dt=F, stack=ctx):
            return stack.enter_context(nc.sbuf_tensor(name, shape, dt))

        def sem(name):
            return ctx.enter_context(nc.semaphore(name))

        resid = sb("resid", [P, NT, D])
        xnT = sb("xnT", [P, 2, KC, NTOK], R)
        regA = sb("regA", [P, 2, 4096], R)
        regC = sb("regC", [P, 2, 4096], R)
        raw16 = sb("raw16", [P, 4096])
        ident = sb("ident", [P, P])
        neg_half = sb("neg_half", [P, 1])
        bz = sb("bz", [P, 2 * MH])
        rden = sb("rden", [P, 2, 4])
        stats = sb("stats", [P, 6])
        meanvar = sb("meanvar", [P, 2])
        vareps = sb("vareps", [P, 1])
        rstd = sb("rstd", [P, 1])
        negmax = sb("negmax", [P, 2, 4])
        rowsum = sb("rowsum", [P, 2, 4])
        rrow = sb("rrow", [P, 2, 4])

        first = ExitStack()
        regB = sb("regB", [P, 2, 4096], R, first)
        rawk = sb("rawk", [P, 4096], F, first)
        sig = sb("sig", [P, 3, HALF], F, first)
        qneg = sb("qneg", [P, HALF], F, first)
        qpos = sb("qpos", [P, HALF], F, first)
        wofold = sb("wofold", [P, 2, KC, P], F, first)
        wofT = sb("wofT", [P, 2, D], R, first)
        memT = sb("memT", [P, 2, P], R, first)
        mem = sb("mem", [P, MH // 2, P], F, first)
        xn = sb("xn", [P, 2, D], F, first)
        kvout = sb("kvout", [P, 2, D], F, first)
        first.close()

        second = ExitStack()
        qT = sb("qT", [P, 2, 8, GH, S], F, second)
        oT = sb("oT", [P, 2, 2, GH, P], R, second)
        wq_raw = sb("wq_raw", [P, KC, 2 * P], F, second)
        k_ring = sb("k_ring", [P, 4, 2, P], F, second)
        v_raw = sb("v_raw", [P, 2, 2, P], F, second)
        v_ring = sb("v_ring", [P, 2, 2, 2, P], R, second)
        probs = sb("probs", [P, 2, 4, P], F, second)
        pT = sb("pT", [P, 2, 2, 4 * P], R, second)
        second.close()
        bank = [ctx.enter_context(nc.psum_tensor(f"bank{i}", [P, 512], F)) for i in range(8)]

        hi_lo = (0, 1)
        ctxT = regA[:, :, :].rearrange("p a (k n) -> p a k n", k=KC)
        sigT = regA[:, :, :].rearrange("p a (m n) -> p a m n", m=MH)
        wq = regA[:, :, :].rearrange("p a (h k n) -> p a h k n", h=GH, k=KC)
        wkv1 = regB[:, :, :].rearrange("p a (w k n) -> p a w k n", w=2, k=KC)
        memwo = regB[:, :, :].rearrange("p a (m n) -> p a m n", m=MH)
        wqaT = regC[:, :, :].rearrange("p a (m k n) -> p a m k n", m=MH, k=KC)
        wkv2 = regC[:, :, :].rearrange("p a (w k n) -> p a w k n", w=2, k=KC)
        wo = regC[:, :, :].rearrange("p a (h n) -> p a h n", h=GH)
        ctx_raw = raw16[:, :].rearrange("p (t n) -> p t n", t=NT)
        woa_raw = raw16[:, :].rearrange("p (r o g n) -> p r o g n", r=2, o=KC, g=GREP)
        wo_raw = raw16[:, :].rearrange("p (h n) -> p h n", h=GH)
        wkv_raw = rawk[:, :].rearrange("p (w k n) -> p w k n", w=2, k=KC)
        wqa_raw = rawk[:, :].rearrange("p (m n) -> p m n", m=MH)
        bz_rows = sig[0:2 * MH, 0, 0:P]
        kv_slots = (kvout[:, 0, :], kvout[:, 1, :], qneg[:, :], qpos[:, :])
        e_xn = raw16[:, 0:2 * D].rearrange("p (r n) -> p r n", r=2)
        e_xnT = raw16[:, 2 * D:4 * D].rearrange("p (r k n) -> p r k n", r=2, k=KC)
        e_out = raw16[:, 4 * D:6 * D].rearrange("p (r n) -> p r n", r=2)
        rout_rows = raw16[0:NE, 5 * D:6 * D]
        expert = raw16[0:NE, 6 * D:7 * D]
        routT = raw16[:, 7 * D:7 * D + KC * NE].rearrange("p (k n) -> p k n", k=KC)
        wq_flat = wq_raw[:, :, :].rearrange("p k n -> p (k n)")
        small = wq_flat[:, 0:10 * NE].rearrange("p (r w n) -> p r w n", r=2, w=5)
        e_wT = wq_flat[0:NE, 10 * NE:10 * NE + 2 * P].rearrange("p (r n) -> p r n", r=2)
        rout_b = wq_flat[:, 14 * NE:15 * NE]
        top = wq_flat[:, 15 * NE:16 * NE].rearrange("p (r w n) -> p r w n", r=2, w=4)

        ctx_loaded = [sem(f"ctx_loaded{i}") for i in range(4)]
        wkv_loaded = [sem("wk_loaded"), sem("wv_loaded")]
        x_loaded = [sem(f"x_loaded{i}") for i in range(4)]
        bz_loaded = sem("bz_loaded")
        mem_loaded = sem("mem_loaded")
        wqa_loaded = [sem(f"wqa_loaded{i}") for i in range(4)]
        woa_loaded = [sem(f"woa_loaded{i}") for i in range(2)]
        expert_loaded = sem("expert_loaded")
        consts_set = sem("consts_set")
        tr_done = sem("tr_done")
        tr_hi = sem("tr_hi")
        tr_used = sem("tr_used")
        mm_done = sem("mm_done")
        mm_act = sem("mm_act")
        mm_dve = sem("mm_dve")
        wkv_hi = sem("wkv_hi")
        wkv_lo = sem("wkv_lo")
        kv_written = [sem(f"kv_written{i}") for i in range(4)]
        dve_step = sem("dve_step")
        var_ready = sem("var_ready")
        rstd_ready = sem("rstd_ready")
        xn_ready = sem("xn_ready")
        qexp_ready = sem("qexp_ready")
        qpos_ready = sem("qpos_ready")
        sig_ready = sem("sig_ready")
        sig_scaled = sem("sig_scaled")
        sig_hi = sem("sig_hi")
        sig_lo = sem("sig_lo")
        spread_done = sem("spread_done")
        den_done = sem("den_done")
        rden_ready = sem("rden_ready")
        fold_half = sem("fold_half")
        fold_done = sem("fold_done")
        y_done = sem("y_done")
        y_used = sem("y_used")
        k_loaded = [sem(f"k_loaded{i}") for i in range(4)]
        v_loaded = [sem(f"v_loaded{i}") for i in range(2)]
        wq_loaded = sem("wq_loaded")
        wo_loaded = sem("wo_loaded")
        wq_hi = sem("wq_hi")
        wq_lo = sem("wq_lo")
        wo_hi = sem("wo_hi")
        wo_lo = sem("wo_lo")
        wo_used = sem("wo_used")
        v_hi = sem("v_hi")
        v_lo = sem("v_lo")
        q_done = sem("q_done")
        q_saved = sem("q_saved")
        scores_done = sem("scores_done")
        negmax_ready = sem("negmax_ready")
        rrow_ready = sem("rrow_ready")
        exp_done = sem("exp_done")
        probs_ready = sem("probs_ready")
        pT_done = sem("pT_done")
        pT_hi = sem("pT_hi")
        pT_lo = sem("pT_lo")
        pv_done = sem("pv_done")
        oT_hi = sem("oT_hi")
        oT_lo = sem("oT_lo")
        proj_done = sem("proj_done")
        proj_added = sem("proj_added")
        routT_done = sem("routT_done")
        routT_ready = sem("routT_ready")
        e_xn_ready = sem("e_xn_ready")
        e_tr_done = sem("e_tr_done")
        e_xnT_ready = sem("e_xnT_ready")
        logits_done = sem("logits_done")
        logits_saved = sem("logits_saved")
        e_max_ready = sem("e_max_ready")
        e_exp_done = sem("e_exp_done")
        e_w_ready = sem("e_w_ready")
        e_wT_done = sem("e_wT_done")
        e_wT_ready = sem("e_wT_ready")
        mix_done = sem("mix_done")
        e_out_ready = sem("e_out_ready")
        out_written = [sem("out_written0"), sem("out_written1")]

        TR_CTX, TR_X, TR_BZ, TR_X2 = 0, 8, 16, 41
        MM_KCTX, MM_VCTX, MM_MEM, MM_VLAT, MM_KLAT, MM_XQ = 0, 8, 16, 40, 48, 56

        def tr_wqa(m):
            return 17 + m if m < 2 else 19 + 3 * (m - 2)

        def tr_mem(m):
            return 20 + 3 * m if m < 6 else 37 + 2 * (m - 6)

        def mm_query(half, m):
            return 32 + m if half else MM_MEM + max(2 * m - 1, 0)

        def mm_memwo(m):
            return MM_MEM + min(2 * m + 2, 15)

        def tr_hi_count(k):
            return k + 1 - (k >= TR_BZ)

        def mm_dve_count(k):
            return min(max(k + 1 - MM_MEM, 0), 24)

        def tr_bank(k):
            return bank[k % 2]

        def mm_bank(k):
            return bank[2 + k % 2]

        den_bank = bank[4]

        def spread_bank(i):
            return bank[5 + i % 2]

        def y_bank(t):
            return bank[4] if t % 2 else bank[7]

        PARTS = ((0, 0), (0, 1), (1, 0))

        block = ctx.enter_context(nc.Block())

        @block.sync
        def _(sp):
            def load_ctx(i):
                sp.dma_start(ctx_raw[:, 2 * i:2 * i + 2, :], ctx_tiles[:, 2 * i:2 * i + 2, :])\
                  .then_inc(ctx_loaded[i], 16)

            def load_wkv(w):
                sp.dma_start(wkv_raw[:, w, :, :], (wk_rows, wv_rows)[w]).then_inc(wkv_loaded[w], 16)

            load_ctx(0)
            load_ctx(1)
            load_wkv(0)
            load_ctx(2)
            load_ctx(3)
            load_wkv(1)
            for i in range(4):
                sp.dma_start(resid[:, 2 * i:2 * i + 2, :], x_tiles[:, 2 * i:2 * i + 2, :])\
                  .then_inc(x_loaded[i], 16)
            sp.dma_start(bz_rows[0:MH, :], bq_rows).then_inc(bz_loaded, 16)
            sp.dma_start(bz_rows[MH:2 * MH, :], attn_z).then_inc(bz_loaded, 16)
            sp.dma_start(mem[:, :, :], mem_heads[:, 0:MH // 2, :]).then_inc(mem_loaded, 16)
            sp.wait_ge(wkv_lo, 2)
            for i in range(4):
                sp.dma_start(wqa_raw[:, 2 * i:2 * i + 2, :], wqa_heads[:, 2 * i:2 * i + 2, :])\
                  .then_inc(wqa_loaded[i], 16)
            sp.wait_ge(tr_done, TR_CTX + NT)
            for m in range(MH):
                if m >= 2:
                    sp.wait_ge(fold_done, m - 1)
                sp.dma_start(woa_raw[:, m % 2, :, :, :].rearrange("p o g n -> p o (g n)"),
                             woa_heads[m]).then_inc(woa_loaded[m % 2], 16)
                if m == 6:
                    sp.wait_ge(tr_done, tr_mem(3) + 1)
                    sp.dma_start(mem[:, :, :], mem_heads[:, MH // 2:MH, :]).then_inc(mem_loaded, 16)
            sp.wait_ge(tr_done, tr_wqa(MH - 1) + 1)
            for w in range(2):
                load_wkv(w)
            sp.wait_ge(fold_done, MH)
            sp.dma_start(wo_raw, wo_rows[:, 0:GH, :]).then_inc(wo_loaded, 16)
            sp.wait_ge(sig_lo, 2 * MH)
            for j in range(4):
                if j:
                    sp.wait_ge(wq_lo, j)
                sp.dma_start(wq_raw[:, :, :], wq_rows[:, :, 2 * j * P:(2 * j + 2) * P]).then_inc(wq_loaded, 16)
            for r in range(4):
                sp.wait_ge(kv_written[r], 16 * 8)

            def load_k(g, t):
                sp.dma_start(k_ring[:, t % 4, :, :],
                             keys_dram[bass.ds(g, 1), :, :, t * P:(t + 1) * P].rearrange("g s d n -> d (g s) n"))\
                  .then_inc(k_loaded[t % 4], 16)

            def load_v(g, t):
                for s in range(2):
                    sp.dma_start(v_raw[s * S:(s + 1) * S, t % 2, :, :],
                                 vals_dram[s, t * P:(t + 1) * P, bass.ds(g * P, P)]
                                 .rearrange("(b s) n -> s b n", b=2)).then_inc(v_loaded[t % 2], 16)

            for t in range(3):
                load_k(0, t)
            for t in range(2):
                load_v(0, t)

            def step(g, t, last, first_step=False):
                n = 8 * g + t
                if not (last and t >= 5):
                    if not first_step:
                        sp.wait_ge(scores_done, 2 * n)
                    load_k(g + (t + 3) // 8, (t + 3) % 8)
                if not (last and t >= 6):
                    sp.wait_ge(v_lo, n + 1)
                    load_v(g + (t + 2) // 8, (t + 2) % 8)
                if last:
                    return
                if t == 1:
                    sp.wait_ge(wo_lo, 8 * g + 8)
                    sp.dma_start(wo_raw, wo_rows[:, bass.ds(8 * g + 8, GH), :]).then_inc(wo_loaded, 16)
                if 1 <= t <= 4:
                    j = t - 1
                    sp.wait_ge(wq_lo, 4 * g + 4 + j)
                    sp.dma_start(wq_raw[:, :, :],
                                 wq_rows[:, :, bass.ds((g + 1) * (GH * P) + 2 * j * P, 2 * P)])\
                      .then_inc(wq_loaded, 16)

            step(0, 0, False, True)
            with sp.Fori(0, KV - 1) as g:
                for t in range(1, NT):
                    step(g, t, False)
                step(g + 1, 0, False)
            def store(t):
                sp.wait_ge(e_out_ready, t + 1)
                sp.dma_start(out_tiles[:, t, :], e_out[:, t % 2, :]).then_inc(out_written[t % 2], 16)

            for t in range(1, NT):
                step(KV - 1, t, True)
                if t >= 3:
                    store(t - 3)
                if t == 1:
                    sp.wait_ge(wo_lo, KV * GH)
                    sp.dma_start(rout_rows, router_w).then_inc(expert_loaded, 16)
                    sp.dma_start(rout_b, router_b.rearrange("(a n) -> a n", a=1).broadcast_to([P, NE]))\
                      .then_inc(expert_loaded, 16)
                    sp.dma_start(expert, expert_b).then_inc(expert_loaded, 16)
            for t in range(NT - 3, NT):
                store(t)
            for r in range(2):
                sp.wait_ge(out_written[r], 16 * NT // 2)

        @block.gpsimd
        def _(pool):
            nc.gpsimd.memset(neg_half[:, :], -0.5).then_inc(consts_set, 1)
            nc.gpsimd.memset(ident[:, :], 0.0).then_inc(consts_set, 1)
            pool.wait_ge(consts_set, 2)
            nc.gpsimd.affine_select(out=ident[:, :], in_=ident[:, :], compare_op=ALU.not_equal, fill=1.0,
                                    base=0, pattern=[[-1, P]], channel_multiplier=1).then_inc(consts_set, 1)

            def root(k):
                pool.wait_ge(var_ready, k + 1)
                nc.gpsimd.tensor_tensor(rstd[:, :], vareps[:, :], neg_half[:, :], ALU.pow)\
                    .then_inc(rstd_ready, 1)

            for t in range(NT):
                root(t)
            for m in range(MH):
                pool.wait_ge(woa_loaded[m % 2], 16 * (m // 2 + 1))
                w = woa_raw[:, m % 2, :, :, :]
                nc.gpsimd.tensor_tensor(w[:, :, 0:2, :], w[:, :, 0:2, :], w[:, :, 2:4, :], ALU.add)\
                    .then_inc(fold_half, 1)
                pool.wait_ge(fold_half, m + 1)
                if m >= 2:
                    pool.wait_ge(tr_done, tr_mem(m - 2) + 2)
                nc.gpsimd.tensor_tensor(wofold[:, m % 2, :, :], w[:, :, 0, :], w[:, :, 1, :], ALU.add)\
                    .then_inc(fold_done, 1)
            for k in range(NT, 3 * NT):
                root(k)

        @block.tensor
        def _(pe):
            pe.wait_ge(consts_set, 3)

            def tr_free(k):
                if k >= 2:
                    pe.wait_ge(tr_used, k - 1)

            def mm_free(k):
                if k >= 2:
                    pe.wait_ge(mm_act, k - 1)
                    if mm_dve_count(k - 2):
                        pe.wait_ge(mm_dve, mm_dve_count(k - 2))

            def transpose_rows(k, rows):
                tr_free(k)
                for c in range(KC):
                    last = nc.tensor.transpose(tr_bank(k)[:, c * P:(c + 1) * P],
                                               rows[:, c * P:(c + 1) * P], ident[:, :])
                last.then_inc(tr_done, 1)

            def product(k, left, right):
                mm_free(k)
                terms = [(a, b, c) for c in range(KC) for a, b in PARTS]
                for i, (a, b, c) in enumerate(terms):
                    last = nc.tensor.matmul(mm_bank(k)[:, :], left(a, c), right(b, c),
                                            start=i == 0, stop=i == len(terms) - 1)
                last.then_inc(mm_done, 1)

            for t in range(NT):
                if t % 2 == 0:
                    pe.wait_ge(ctx_loaded[t // 2], 16)
                transpose_rows(TR_CTX + t, ctx_raw[:, t, :])

            def keys(base, wkv, srcT, half):
                for g in range(KV):
                    product(base + KV * half + g,
                            lambda a, c: wkv[:, a, 0, c, g * P:(g + 1) * P],
                            lambda b, c: srcT[:, b, c, half * HALF:(half + 1) * HALF])

            def values(k, wkv, srcT, t):
                product(k, lambda a, c: srcT[:, a, c, t * P:(t + 1) * P],
                        lambda b, c: wkv[:, b, 1, c, :])

            pe.wait_ge(tr_used, TR_CTX + 4)
            pe.wait_ge(wkv_lo, 1)
            keys(MM_KCTX, wkv1, ctxT, 0)
            pe.wait_ge(tr_used, TR_CTX + NT)
            keys(MM_KCTX, wkv1, ctxT, 1)
            pe.wait_ge(wkv_lo, 2)
            for t in range(NT):
                values(MM_VCTX + t, wkv1, ctxT, t)
                pe.wait_ge(xn_ready, t + 1)
                transpose_rows(TR_X + t, xn[:, t % 2, :])

            pe.wait_ge(bz_loaded, 32)
            tr_free(TR_BZ)
            nc.tensor.transpose(tr_bank(TR_BZ)[:, 0:2 * MH], bz_rows, ident[0:2 * MH, 0:2 * MH])\
                .then_inc(tr_done, 1)

            def memory_wq(m):
                if m % 2 == 0:
                    pe.wait_ge(wqa_loaded[m // 2], 16)
                transpose_rows(tr_wqa(m), wqa_raw[:, m, :])

            def memory_query(half, m):
                if half == 0:
                    pe.wait_ge(tr_used, tr_wqa(m) + 1)
                product(mm_query(half, m),
                        lambda a, c: wqaT[:, a, m, c, :],
                        lambda b, c: xnT[:, b, c, half * HALF:(half + 1) * HALF])

            def denominators(half, m):
                i = half * MH + m
                pe.wait_ge(sig_ready, i + 1)
                if i:
                    pe.wait_ge(rden_ready, i)
                if i == MH:
                    pe.wait_ge(y_used, 4)
                for tt in range(4):
                    last = nc.tensor.matmul(den_bank[:, tt:tt + 1], sig[:, i % 3, tt * P:(tt + 1) * P],
                                            bz[:, MH + m:MH + m + 1], start=True, stop=True)
                last.then_inc(den_done, 1)

            def spread(half, m):
                i = half * MH + m
                pe.wait_ge(rden_ready, i + 1)
                if i >= 2:
                    pe.wait_ge(sig_scaled, i - 1)
                for tt in range(4):
                    last = nc.tensor.transpose(spread_bank(i)[:, tt * P:(tt + 1) * P],
                                               rden[:, i % 2, tt:tt + 1].broadcast_to([P, P]), ident[:, :])
                last.then_inc(spread_done, 1)

            def memory_transposes(m):
                k = tr_mem(m)
                if m % 4 == 0:
                    pe.wait_ge(mem_loaded, 16 * (m // 4 + 1))
                tr_free(k)
                nc.tensor.transpose(tr_bank(k)[:, 0:P], mem[:, m % 4, :], ident[:, :]).then_inc(tr_done, 1)

            def wo_transposes(m):
                k = tr_mem(m) + 1
                pe.wait_ge(fold_done, m + 1)
                tr_free(k)
                for c in range(KC):
                    last = nc.tensor.transpose(tr_bank(k)[:, c * P:(c + 1) * P],
                                               wofold[:, m % 2, c, :], ident[:, :])
                last.then_inc(tr_done, 1)

            def memory_weights(m):
                k = mm_memwo(m)
                mm_free(k)
                pe.wait_ge(tr_used, tr_mem(m) + 2)
                for i, (a, b) in enumerate(PARTS):
                    last = nc.tensor.matmul(mm_bank(k)[:, :], memT[:, a, :], wofT[:, b, :],
                                            start=i == 0, stop=i == 2)
                last.then_inc(mm_done, 1)

            memory_wq(0)
            memory_wq(1)

            def memory_heads(half):
                for m in range(MH + 2):
                    if m < MH:
                        memory_query(half, m)
                    if half == 0 and m + 2 < MH:
                        memory_wq(m + 2)
                    if 1 <= m <= MH:
                        denominators(half, m - 1)
                        if half == 0:
                            memory_weights(m - 1)
                    if half == 0 and m < MH:
                        memory_transposes(m)
                    if m >= 2:
                        spread(half, m - 2)
                    if half == 0 and m < MH:
                        wo_transposes(m)

            def memory_output(half):
                for t in range(4 * half, 4 * half + 4):
                    if t >= 2:
                        pe.wait_ge(y_used, t - 1)
                    for m in range(MH):
                        if t % 4 == 0:
                            pe.wait_ge(sig_lo, half * MH + m + 1)
                        if t == 0:
                            pe.wait_ge(mm_dve, mm_dve_count(mm_memwo(m)))
                        for i, (a, b) in enumerate(PARTS):
                            last = nc.tensor.matmul(y_bank(t)[:, :],
                                                    sigT[:, a, m, (t % 4) * P:(t % 4 + 1) * P],
                                                    memwo[:, b, m, :], start=m == 0 and i == 0,
                                                    stop=m == MH - 1 and i == 2)
                    last.then_inc(y_done, 1)
                    if t % 4:
                        latent_transposes(t - 1)

            def latent_transposes(t):
                pe.wait_ge(xn_ready, NT + t + 1)
                transpose_rows(TR_X2 + t, xn[:, t % 2, :])

            memory_heads(0)
            pe.wait_ge(rden_ready, MH)
            memory_output(0)
            memory_heads(1)
            latent_transposes(3)
            pe.wait_ge(rden_ready, 2 * MH)
            memory_output(1)
            pe.wait_ge(wkv_lo, 4)
            for t in range(4):
                values(MM_VLAT + t, wkv2, xnT, t)
            latent_transposes(7)
            for t in range(4, NT):
                pe.wait_ge(tr_used, TR_X2 + t + 1)
                values(MM_VLAT + t, wkv2, xnT, t)
            for half in range(2):
                keys(MM_KLAT, wkv2, xnT, half)

            def queries(k_bank, head, half, done):
                for i, (c, (a, b)) in enumerate((c, ab) for c in range(KC) for ab in PARTS):
                    last = nc.tensor.matmul(k_bank[:, :], wq[:, a, head, c, :],
                                            xnT[:, b, c, half * HALF:(half + 1) * HALF],
                                            start=i == 0, stop=i == 3 * KC - 1)
                last.then_inc(done, 1)

            for h in range(GH):
                k = MM_XQ + h
                mm_free(k)
                if h % 2 == 0:
                    pe.wait_ge(wq_lo, h // 2 + 1)
                queries(mm_bank(k), h, 0, mm_done)

            def project(g, t, parity, release):
                n = 8 * g + t
                pe.wait_ge(oT_lo, 2 * n + 2)
                pe.wait_ge(proj_added, n + 1)
                for h in range(GH):
                    if t == 0:
                        pe.wait_ge(wo_lo, 8 * g + h + 1)
                    for i, (a, b) in enumerate(PARTS):
                        last = nc.tensor.matmul(bank[7][:, :], oT[:, parity, a, h, :], wo[:, b, h, :],
                                                start=h == 0 and i == 0, stop=h == GH - 1 and i == 2)
                    if release and h < GH - 1:
                        last.then_inc(wo_used, 1)
                last.then_inc(proj_done, 1)

            attended = 2 * KV * NT

            def expert_first(t):
                n = 8 * (KV - 1) + t
                if t == 2:
                    pe.wait_ge(expert_loaded, 48)
                    pe.wait_ge(oT_lo, 2 * n)
                    for c in range(KC):
                        last = nc.tensor.transpose(bank[5][:, c * NE:(c + 1) * NE],
                                                   rout_rows[:, c * P:(c + 1) * P], ident[0:NE, 0:NE])
                    last.then_inc(routT_done, 1)
                if 2 <= t < NT + 2:
                    e = t - 2
                    pe.wait_ge(e_xn_ready, e + 1)
                    pe.wait_ge(oT_lo, min(2 * n - 1, attended))
                    if e:
                        pe.wait_ge(e_xnT_ready, e)
                    for c in range(KC):
                        last = nc.tensor.transpose(bank[4][:, c * P:(c + 1) * P],
                                                   e_xn[:, e % 2, c * P:(c + 1) * P], ident[:, :])
                    last.then_inc(e_tr_done, 1)
                if t >= 3:
                    e = t - 3
                    pe.wait_ge(e_w_ready, e + 1)
                    pe.wait_ge(exp_done, min(2 * n + 2, attended))
                    if e:
                        pe.wait_ge(e_wT_ready, e)
                    nc.tensor.transpose(bank[1][0:NE, 0:P], small[:, e % 2, 4, :], ident[:, :])\
                        .then_inc(e_wT_done, 1)

            def expert_second(t):
                n = 8 * (KV - 1) + t
                if 2 <= t < NT + 2:
                    e = t - 2
                    pe.wait_ge(e_xnT_ready, e + 1)
                    pe.wait_ge(oT_lo, min(2 * n, attended))
                    if e:
                        pe.wait_ge(logits_saved, e)
                    else:
                        pe.wait_ge(routT_ready, 1)
                    for c in range(KC):
                        last = nc.tensor.matmul(bank[5][:, 0:NE], e_xnT[:, e % 2, c, :], routT[:, c, :],
                                                start=c == 0, stop=c == KC - 1)
                    last.then_inc(logits_done, 1)
                if t >= 3:
                    e = t - 3
                    pe.wait_ge(e_wT_ready, e + 1)
                    pe.wait_ge(exp_done, min(2 * n + 1, attended))
                    if e:
                        pe.wait_ge(e_out_ready, e)
                    nc.tensor.matmul(bank[0][:, :], e_wT[:, e % 2, :], expert[:, :], start=True, stop=True)\
                        .then_inc(mix_done, 1)

            def step(g, t, last_group, first_step=False):
                n = 8 * g + t
                half = t // 4
                if first_step:
                    pe.wait_ge(mm_act, MM_XQ + GH)
                    pe.wait_ge(tr_used, TR_X2 + NT)
                elif t % 4 == 0:
                    pe.wait_ge(q_saved, 16 * g + 2 * t)
                pe.wait_ge(k_loaded[t % 4], 16 * (2 * g + half + 1))
                for bb in range(2):
                    if last_group and t >= 4:
                        pe.wait_ge((e_out_ready, e_wT_ready)[bb], t - 3)
                    if not first_step:
                        pe.wait_ge(exp_done, 2 * n - 1 + bb)
                    for p in range(4):
                        last = nc.tensor.matmul(bank[bb][:, p * P:(p + 1) * P],
                                                qT[:, half, (2 * t + bb) % 8, 2 * p:2 * p + 2, :]
                                                .rearrange("p h s -> p (h s)"),
                                                k_ring[:, t % 4, :, bb * S:(bb + 1) * S],
                                                start=True, stop=True)
                    last.then_inc(scores_done, 1)

                def next_queries(u):
                    if last_group and t >= 4:
                        return
                    k = 16 * g + 2 * t + u
                    if first_step and u == 0:
                        pe.wait_ge(sig_scaled, 2 * MH)
                    else:
                        pe.wait_ge(q_saved, k)
                    head = 2 * (t % 4) + u
                    if t >= 4 and u == 0:
                        pe.wait_ge(wq_lo, 4 * g + 4 + t - 3)
                    queries(bank[6], head, 1 - half, q_done)

                next_queries(0)
                if not first_step:
                    if t == 0:
                        project(g - 1, 7, 1, True)
                    else:
                        project(g, t - 1, (t - 1) % 2, False)
                if last_group:
                    expert_first(t)
                for bb in range(2):
                    pe.wait_ge(probs_ready, 2 * n + bb + 1)
                    if not first_step:
                        pe.wait_ge(pT_lo, 2 * n - 1 + bb)
                    for p in range(4):
                        last = nc.tensor.transpose(bank[2 + bb][:, p * P:(p + 1) * P],
                                                   probs[:, bb, p, :], ident[:, :])
                    last.then_inc(pT_done, 1)
                if last_group:
                    expert_second(t)
                next_queries(1)
                pe.wait_ge(v_lo, n + 1)
                for bb in range(2):
                    pe.wait_ge(pT_lo, 2 * n + bb + 1)
                    if first_step:
                        pe.wait_ge(y_used, NT)
                    else:
                        pe.wait_ge(oT_lo, 2 * n - 1 + bb)
                    if last_group and t >= 2:
                        pe.wait_ge((e_xnT_ready, logits_saved)[bb], t - 1)
                    for i, (a, b) in enumerate(PARTS):
                        last = nc.tensor.matmul(bank[4 + bb][:, :], v_ring[:, t % 2, bb, a, :],
                                                pT[:, bb, b, :], start=i == 0, stop=i == 2)
                    last.then_inc(pv_done, 1)

            step(0, 0, False, True)
            with pe.Fori(0, KV - 1) as g:
                for t in range(1, NT):
                    step(g, t, False)
                step(g + 1, 0, False)
            for t in range(1, NT):
                step(KV - 1, t, True)
            project(KV - 1, NT - 1, 1, False)

            for t in range(NT, NT + 3):
                expert_first(t)
                expert_second(t)

        @block.scalar
        def _(act):
            def high(dst, src):
                return nc.scalar.copy(dst, src)

            def wq_high(g, j):
                act.wait_ge(wq_loaded, 16 * (4 * g + j + 1))
                high(wq[:, 0, 2 * j:2 * j + 2, :, :],
                     wq_raw[:, :, :].rearrange("p k (h n) -> p h k n", h=2)).then_inc(wq_hi, 1)

            def v_high(g, t):
                act.wait_ge(v_loaded[t % 2], 32 * (4 * g + t // 2 + 1))
                high(v_ring[:, t % 2, :, 0, :], v_raw[:, t % 2, :, :]).then_inc(v_hi, 1)

            def wo_high(g, h):
                high(wo[:, 0, h, :], wo_raw[:, h, :]).then_inc(wo_hi, 1)

            def save_queries(k_bank, half, head, saved):
                nc.scalar.mul(qT[:, half, :, head, :], k_bank[:, :].rearrange("p (b s) -> p b s", b=8), SCALE)\
                    .then_inc(saved, 1)

            def tr_high(k, dst, src=None):
                act.wait_ge(tr_done, k + 1)
                high(dst, tr_bank(k)[:, :] if src is None else src).then_inc(tr_hi, 1)

            def blocks(k):
                return tr_bank(k)[:, :].rearrange("p (c n) -> p c n", c=KC)

            def wkv_high(w):
                act.wait_ge(wkv_loaded[w], 16)
                for c in range(KC):
                    high(wkv1[:, 0, w, c, :], wkv_raw[:, w, c, :]).then_inc(wkv_hi, 1)

            for t in range(NT):
                tr_high(TR_CTX + t, ctxT[:, 0, :, t * P:(t + 1) * P], blocks(TR_CTX + t))
                if t == 3:
                    wkv_high(0)

            def save_kv(k, n, dst):
                act.wait_ge(mm_done, k + 1)
                if n >= 4:
                    act.wait_ge(kv_written[n % 4], 16 * (n // 4))
                nc.scalar.copy(kv_slots[n % 4], mm_bank(k)[:, :]).then_inc(mm_act, 1)
                act.wait_ge(mm_act, k + 1)
                act.dma_start(dst, kv_slots[n % 4]).then_inc(kv_written[n % 4], 16)

            def save_keys(base, n, s, half):
                for g in range(KV):
                    i = KV * half + g
                    save_kv(base + i, n + i, keys_dram[g, s, :, half * HALF:(half + 1) * HALF])

            save_keys(MM_KCTX, 0, 0, 0)
            wkv_high(1)
            save_keys(MM_KCTX, 0, 0, 1)
            for t in range(NT):
                save_kv(MM_VCTX + t, 8 + t, vals_dram[0, t * P:(t + 1) * P, :])
                tr_high(TR_X + t, xnT[:, 0, :, t * P:(t + 1) * P], blocks(TR_X + t))

            def memory_wq(m):
                tr_high(tr_wqa(m), wqaT[:, 0, m, :, :], blocks(tr_wqa(m)))

            memory_wq(0)
            memory_wq(1)

            def memory_heads(half):
                for m in range(MH + 2):
                    if half == 0 and m + 2 < MH:
                        memory_wq(m + 2)
                    if m < MH:
                        k = mm_query(half, m)
                        act.wait_ge(mm_dve, mm_dve_count(k))
                        nc.scalar.activation(qneg[:, :], qneg[:, :], ACT.Exp).then_inc(qexp_ready, 1)
                        i = half * MH + m
                        if i:
                            act.wait_ge(sig_ready, i)
                        nc.scalar.activation(qpos[:, :], mm_bank(k)[:, :], ACT.Relu, bias=bz[:, m:m + 1])\
                            .then_inc(mm_act, 1)
                    if half == 0 and 1 <= m <= MH:
                        act.wait_ge(mm_done, mm_memwo(m - 1) + 1)
                        high(memwo[:, 0, m - 1, :], mm_bank(mm_memwo(m - 1))[:, :]).then_inc(mm_act, 1)
                    if half == 0 and m < MH:
                        tr_high(tr_mem(m), memT[:, 0, :], tr_bank(tr_mem(m))[:, 0:P])
                        tr_high(tr_mem(m) + 1, wofT[:, 0, :])
                    if m >= 2:
                        act.wait_ge(sig_scaled, half * MH + m - 1)
                        high(sigT[:, 0, m - 2, :], sig[:, (half * MH + m - 2) % 3, :]).then_inc(sig_hi, 1)

            act.wait_ge(tr_used, TR_BZ + 1)
            for r in range(4):
                act.wait_ge(kv_written[r], 16 * 4)
            memory_heads(0)

            def latent_high(t):
                tr_high(TR_X2 + t, xnT[:, 0, :, t * P:(t + 1) * P], blocks(TR_X2 + t))

            for t in range(3):
                latent_high(t)
            act.wait_ge(y_done, 4)
            memory_heads(1)
            for w in range(2):
                act.wait_ge(wkv_loaded[w], 32)
                for c in range(KC):
                    high(wkv2[:, 0, w, c, :], wkv_raw[:, w, c, :]).then_inc(wkv_hi, 1)
            for t in range(3, 7):
                latent_high(t)
            def save_latent_values(t):
                save_kv(MM_VLAT + t, 16 + t, vals_dram[1, t * P:(t + 1) * P, :])
                if t in (2, 5):
                    act.wait_ge(y_done, NT)
                    wq_high(0, t // 3)

            for t in range(4):
                save_latent_values(t)
            latent_high(7)
            for t in range(4, NT):
                save_latent_values(t)
            for half in range(2):
                save_keys(MM_KLAT, 24, 1, half)
                wq_high(0, 2 + half)
            for h in range(GH):
                k = MM_XQ + h
                act.wait_ge(mm_done, k + 1)
                save_queries(mm_bank(k), 0, h, mm_act)
                if h == 0:
                    act.wait_ge(wo_loaded, 16)
                wo_high(0, h)
                if h == 5:
                    v_high(0, 0)

            def expert_first(t):
                if 2 <= t < NT + 2:
                    e = t - 2
                    act.wait_ge(e_tr_done, e + 1)
                    if e >= 2:
                        act.wait_ge(logits_done, e - 1)
                    nc.scalar.copy(e_xnT[:, e % 2, :, :], bank[4][:, :].rearrange("p (k n) -> p k n", k=KC))\
                        .then_inc(e_xnT_ready, 1)
                if t >= 3:
                    e = t - 3
                    act.wait_ge(e_wT_done, e + 1)
                    if e >= 2:
                        act.wait_ge(mix_done, e - 1)
                    nc.scalar.copy(e_wT[:, e % 2, :], bank[1][0:NE, 0:P]).then_inc(e_wT_ready, 1)

            def expert_second(t):
                if 2 <= t < NT + 2:
                    e = t - 2
                    act.wait_ge(e_max_ready, e + 1)
                    nc.scalar.activation(small[:, e % 2, 1, :], small[:, e % 2, 0, :], ACT.Exp,
                                         bias=top[:, e % 2, 1, 0:1], accum_out=top[:, e % 2, 2, 0:1])\
                        .then_inc(e_exp_done, 1)

            def step(g, t, last_group, first_step=False):
                n = 8 * g + t
                half = t // 4
                for bb in range(2):
                    act.wait_ge(negmax_ready, 2 * n + bb + 1)
                    if not first_step:
                        act.wait_ge(pT_done, 2 * n - 1 + bb)
                    for p in range(4):
                        last = nc.scalar.activation(probs[:, bb, p, :], bank[bb][:, p * P:(p + 1) * P], ACT.Exp,
                                                    bias=negmax[:, bb, p:p + 1],
                                                    accum_out=rowsum[:, bb, p:p + 1])
                    last.then_inc(exp_done, 1)

                def save_next(u):
                    if last_group and t >= 4:
                        return
                    act.wait_ge(q_done, 16 * g + 2 * t + u + 1)
                    save_queries(bank[6], 1 - half, 2 * (t % 4) + u, q_saved)

                save_next(0)
                if not (last_group and t == 7):
                    if not first_step:
                        act.wait_ge(pv_done, 2 * n)
                    v_high(g, t + 1)
                if not last_group and 2 <= t <= 5:
                    act.wait_ge(q_done, 16 * g + 2 * (t - 2) + 2)
                    wq_high(g + 1, t - 2)
                if t == 0 and not first_step:
                    act.wait_ge(wo_loaded, 16 * g + 16)
                    for h in range(GH):
                        if h < GH - 1:
                            act.wait_ge(wo_used, (GH - 1) * (g - 1) + h + 1)
                        else:
                            act.wait_ge(proj_done, 8 * g)
                        wo_high(g, h)
                if last_group:
                    expert_first(t)
                for bb in range(2):
                    act.wait_ge(pT_done, 2 * n + bb + 1)
                    if not first_step:
                        act.wait_ge(pv_done, 2 * n - 1 + bb)
                    high(pT[:, bb, 0, :], bank[2 + bb][:, :]).then_inc(pT_hi, 1)
                if last_group:
                    expert_second(t)
                save_next(1)
                for bb in range(2):
                    act.wait_ge(pv_done, 2 * n + bb + 1)
                    high(oT[:, t % 2, 0, :, bb * S:(bb + 1) * S],
                         bank[4 + bb][:, :].rearrange("p (h s) -> p h s", h=GH)).then_inc(oT_hi, 1)

            step(0, 0, False, True)
            with act.Fori(0, KV - 1) as g:
                for t in range(1, NT):
                    step(g, t, False)
                step(g + 1, 0, False)
            for t in range(1, NT):
                step(KV - 1, t, True)

            for t in range(NT, NT + 3):
                expert_first(t)
                expert_second(t)

        @block.vector
        def _(dve):
            steps = [0]

            def settled(ins):
                steps[0] += 1
                ins.then_inc(dve_step, 1)
                dve.wait_ge(dve_step, steps[0])

            def low(dst, src, high):
                return nc.vector.tensor_tensor(dst, src, high.bitcast(F), ALU.subtract)

            def blocks(k):
                return tr_bank(k)[:, :].rearrange("p (c n) -> p c n", c=KC)

            def tr_low(k, dst, src, high):
                dve.wait_ge(tr_hi, tr_hi_count(k))
                low(dst, src, high).then_inc(tr_used, 1)

            def normalise(k, src, dst, done):
                settled(nc.vector.bn_stats(stats[:, :], src))
                settled(nc.vector.bn_aggr(meanvar[:, :], stats[:, :]))
                nc.vector.tensor_scalar(vareps[:, :], meanvar[:, 1:2], LN_EPS, None, ALU.add)\
                    .then_inc(var_ready, 1)
                dve.wait_ge(rstd_ready, k + 1)
                nc.vector.tensor_scalar(dst, src, meanvar[:, 0:1], rstd[:, 0:1],
                                        ALU.subtract, ALU.mult).then_inc(done, 1)

            def wkv_low(w, wkv, n):
                for c in range(KC):
                    dve.wait_ge(wkv_hi, n + c + 1)
                    last = low(wkv[:, 1, w, c, :], wkv_raw[:, w, c, :], wkv[:, 0, w, c, :])
                last.then_inc(wkv_lo, 1)

            for t in range(NT):
                cols = slice(t * P, (t + 1) * P)
                tr_low(TR_CTX + t, ctxT[:, 1, :, cols], blocks(TR_CTX + t), ctxT[:, 0, :, cols])
                if t == 3:
                    wkv_low(0, wkv1, 0)
            wkv_low(1, wkv1, KC)

            def norm_x(t):
                if t % 2 == 0:
                    dve.wait_ge(x_loaded[t // 2], 16)
                if t >= 2:
                    dve.wait_ge(tr_done, TR_X + t - 1)
                normalise(t, resid[:, t, :], xn[:, t % 2, :], xn_ready)

            def x_low(base, t):
                cols = slice(t * P, (t + 1) * P)
                tr_low(base + t, xnT[:, 1, :, cols], blocks(base + t), xnT[:, 0, :, cols])

            norm_x(0)
            for t in range(NT):
                if t + 1 < NT:
                    norm_x(t + 1)
                x_low(TR_X, t)
            dve.wait_ge(tr_done, TR_BZ + 1)
            nc.vector.tensor_copy(bz[:, :], tr_bank(TR_BZ)[:, 0:2 * MH]).then_inc(tr_used, 1)
            dve.wait_ge(tr_used, TR_BZ + 1)

            def memory_wq(m):
                tr_low(tr_wqa(m), wqaT[:, 1, m, :, :], blocks(tr_wqa(m)), wqaT[:, 0, m, :, :])

            memory_wq(0)
            memory_wq(1)

            def memory_heads(half):
                for m in range(MH + 2):
                    i = half * MH + m
                    if m < MH:
                        k = mm_query(half, m)
                        if i:
                            dve.wait_ge(sig_ready, i)
                        dve.wait_ge(mm_done, k + 1)
                        nc.vector.tensor_scalar(qneg[:, :], mm_bank(k)[:, :], bz[:, m:m + 1], 0.0,
                                                ALU.add, ALU.min).then_inc(mm_dve, 1)
                    if half == 0 and m + 2 < MH:
                        memory_wq(m + 2)
                    if 1 <= m <= MH:
                        dve.wait_ge(den_done, i)
                        if i >= 3:
                            dve.wait_ge(spread_done, i - 2)
                        r = rden[:, (i - 1) % 2, :]
                        settled(nc.vector.tensor_scalar(r, den_bank[:, 0:4], DEN_EPS, None, ALU.add))
                        nc.vector.reciprocal(r, r).then_inc(rden_ready, 1)
                    if half == 0 and 1 <= m <= MH:
                        k = mm_memwo(m - 1)
                        dve.wait_ge(mm_act, k + 1)
                        low(memwo[:, 1, m - 1, :], mm_bank(k)[:, :], memwo[:, 0, m - 1, :]).then_inc(mm_dve, 1)
                    if m >= 2:
                        old = sig[:, (i - 2) % 3, :]
                        dve.wait_ge(spread_done, i - 1)
                        nc.vector.tensor_tensor(old, old, spread_bank(i - 2)[:, :], ALU.mult)\
                            .then_inc(sig_scaled, 1)
                    if m < MH:
                        dve.wait_ge(mm_act, mm_query(half, m) + 1)
                        nc.vector.tensor_tensor(sig[:, i % 3, :], qneg[:, :], qpos[:, :], ALU.add)\
                            .then_inc(sig_ready, 1)
                    if half == 0 and m < MH:
                        k = tr_mem(m)
                        tr_low(k, memT[:, 1, :], tr_bank(k)[:, 0:P], memT[:, 0, :])
                        tr_low(k + 1, wofT[:, 1, :], tr_bank(k + 1)[:, :], wofT[:, 0, :])
                    if m >= 2:
                        dve.wait_ge(sig_hi, i - 1)
                        low(sigT[:, 1, m - 2, :], old, sigT[:, 0, m - 2, :]).then_inc(sig_lo, 1)

            for r in range(4):
                dve.wait_ge(kv_written[r], 16 * 4)
            memory_heads(0)

            def add_memory(t):
                dve.wait_ge(y_done, t + 1)
                nc.vector.tensor_tensor(resid[:, t, :], resid[:, t, :], y_bank(t)[:, :], ALU.add)\
                    .then_inc(y_used, 1)
                dve.wait_ge(y_used, t + 1)
                if t >= 2:
                    dve.wait_ge(tr_done, TR_X2 + t - 1)
                normalise(NT + t, resid[:, t, :], xn[:, t % 2, :], xn_ready)

            for t in range(4):
                add_memory(t)
                if t:
                    x_low(TR_X2, t - 1)
            memory_heads(1)
            for w in range(2):
                wkv_low(w, wkv2, (2 + w) * KC)
            x_low(TR_X2, 3)
            for t in range(4, NT):
                add_memory(t)
                if t > 4:
                    x_low(TR_X2, t - 1)
            x_low(TR_X2, 7)

            def wq_low(g, j):
                dve.wait_ge(wq_hi, 4 * g + j + 1)
                low(wq[:, 1, 2 * j:2 * j + 2, :, :], wq_raw[:, :, :].rearrange("p k (h n) -> p h k n", h=2),
                    wq[:, 0, 2 * j:2 * j + 2, :, :]).then_inc(wq_lo, 1)

            def v_low(g, t):
                dve.wait_ge(v_hi, 8 * g + t + 1)
                low(v_ring[:, t % 2, :, 1, :], v_raw[:, t % 2, :, :], v_ring[:, t % 2, :, 0, :]).then_inc(v_lo, 1)

            def wo_low(g, h):
                dve.wait_ge(wo_hi, 8 * g + h + 1)
                low(wo[:, 1, h, :], wo_raw[:, h, :], wo[:, 0, h, :]).then_inc(wo_lo, 1)

            for j in range(4):
                wq_low(0, j)
            for h in range(GH):
                wo_low(0, h)
                if h == 5:
                    v_low(0, 0)
            nc.vector.tensor_copy(stats[:, 0:1], meanvar[:, 0:1]).then_inc(proj_added, 1)

            def expert_norm(t):
                if 2 <= t < NT + 2:
                    e = t - 2
                    dve.wait_ge(proj_added, 8 * (KV - 1) + e + 2)
                    if e >= 2:
                        dve.wait_ge(e_tr_done, e - 1)
                    normalise(2 * NT + e, resid[:, e, :], e_xn[:, e % 2, :], e_xn_ready)

            def expert_rest(t):
                if t == 2:
                    dve.wait_ge(routT_done, 1)
                    nc.vector.tensor_copy(routT, bank[5][:, 0:KC * NE].rearrange("p (k n) -> p k n", k=KC))\
                        .then_inc(routT_ready, 1)
                if 2 <= t < NT + 2:
                    e = t - 2
                    r = e % 2
                    logits, expd, score, rest, weight = (small[:, r, i, :] for i in range(5))
                    dve.wait_ge(logits_done, e + 1)
                    nc.vector.tensor_tensor(logits, bank[5][:, 0:NE], rout_b, ALU.add)\
                        .then_inc(logits_saved, 1)
                    dve.wait_ge(logits_saved, e + 1)
                    settled(nc.vector.max(top[:, r, 0, :], logits))
                    nc.vector.tensor_scalar(top[:, r, 1, 0:1], top[:, r, 0, 0:1], -1.0, None, ALU.mult)\
                        .then_inc(e_max_ready, 1)
                if t >= 3:
                    p = t - 3
                    if p >= 2:
                        dve.wait_ge(out_written[p % 2], 16 * (p // 2))
                    settled(nc.vector.scalar_tensor_tensor(out=e_out[:, p % 2, :], in0=e_xn[:, p % 2, :],
                                                           scalar=top[:, p % 2, 2, 2:3], in1=resid[:, p, :],
                                                           op0=ALU.mult, op1=ALU.add))
                    dve.wait_ge(mix_done, p + 1)
                    nc.vector.tensor_tensor(e_out[:, p % 2, :], e_out[:, p % 2, :], bank[0][:, :], ALU.add)\
                        .then_inc(e_out_ready, 1)
                if 2 <= t < NT + 2:
                    dve.wait_ge(e_exp_done, e + 1)
                    settled(nc.vector.reciprocal(top[:, r, 2, 1:2], top[:, r, 2, 0:1]))
                    settled(nc.vector.tensor_scalar(score, expd, top[:, r, 2, 1:2], None, ALU.mult))
                    settled(nc.vector.max(top[:, r, 3, :], score))
                    nc.vector.tensor_reduce(top[:, r, 2, 2:3], top[:, r, 3, :], axis=AX, op=ALU.add)
                    settled(nc.vector.match_replace(rest, top[:, r, 3, :], score, 0.0))
                    nc.vector.tensor_tensor(weight, score, rest, ALU.subtract).then_inc(e_w_ready, 1)

            def step(g, t, last_group, first_step=False):
                n = 8 * g + t
                for bb in range(2):
                    dve.wait_ge(scores_done, 2 * n + bb + 1)
                    nc.vector.tensor_reduce(negmax[:, bb, :], bank[bb][:, :].rearrange("p (c n) -> p c n", c=4),
                                            axis=AX, op=ALU.max, negate=True).then_inc(negmax_ready, 1)
                if last_group:
                    expert_norm(t)
                for bb in range(2):
                    dve.wait_ge(exp_done, 2 * n + bb + 1)
                    nc.vector.reciprocal(rrow[:, bb, :], rowsum[:, bb, :]).then_inc(rrow_ready, 1)
                    dve.wait_ge(rrow_ready, 2 * n + bb + 1)
                    nc.vector.tensor_tensor(probs[:, bb, :, :], probs[:, bb, :, :],
                                            rrow[:, bb, :].unsqueeze(2).broadcast_to([P, 4, P]),
                                            ALU.mult).then_inc(probs_ready, 1)
                if not (last_group and t == 7):
                    v_low(g, t + 1)
                if not last_group and 2 <= t <= 5:
                    wq_low(g + 1, t - 2)
                if t == 0 and not first_step:
                    for h in range(GH):
                        wo_low(g, h)
                if not first_step:
                    dve.wait_ge(proj_done, n)
                    rows = resid[:, (t - 1) % NT, :]
                    nc.vector.tensor_tensor(rows, rows, bank[7][:, :], ALU.add).then_inc(proj_added, 1)
                for bb in range(2):
                    dve.wait_ge(pT_hi, 2 * n + bb + 1)
                    low(pT[:, bb, 1, :], bank[2 + bb][:, :], pT[:, bb, 0, :]).then_inc(pT_lo, 1)
                if last_group:
                    expert_rest(t)
                for bb in range(2):
                    dve.wait_ge(oT_hi, 2 * n + bb + 1)
                    cols = slice(bb * S, (bb + 1) * S)
                    low(oT[:, t % 2, 1, :, cols], bank[4 + bb][:, :].rearrange("p (h s) -> p h s", h=GH),
                        oT[:, t % 2, 0, :, cols]).then_inc(oT_lo, 1)

            step(0, 0, False, True)
            with dve.Fori(0, KV - 1) as g:
                for t in range(1, NT):
                    step(g, t, False)
                step(g + 1, 0, False)
            for t in range(1, NT):
                step(KV - 1, t, True)
            for t in range(NT, NT + 3):
                if t == NT:
                    dve.wait_ge(proj_done, KV * NT)
                    nc.vector.tensor_tensor(resid[:, 7, :], resid[:, 7, :], bank[7][:, :], ALU.add)\
                        .then_inc(proj_added, 1)
                expert_norm(t)
                expert_rest(t)


_INS = ["x", "ctx_4096", "L0_attn_Wq", "L0_attn_bq", "L0_attn_Wo", "L0_attn_M", "L0_attn_z",
        "L0_xattn_Wq", "L0_xattn_Wk", "L0_xattn_Wv", "L0_xattn_Wo",
        "L0_ffn_router_weight", "L0_ffn_router_bias", "L0_ffn_expert_bias"]


def kernel(**inputs):
    import numpy as _np
    import concourse.bacc as _bacc
    from concourse import mybir as _mybir
    from concourse.bass_utils import run_bass_kernel_spmd as _run

    nc = _bacc.Bacc("TRN2", target_bir_lowering=False, num_devices=1)
    arrays, args = {}, []
    for name in _INS:
        a = _np.ascontiguousarray(inputs[name])
        arrays[f"in_{name}"] = a
        args.append(nc.dram_tensor(f"in_{name}", a.shape, _mybir.dt.from_np(a.dtype), kind="ExternalInput").ap())
    shape = inputs["x"].shape
    args.append(nc.dram_tensor("out_x", shape, _mybir.dt.float32, kind="ExternalOutput").ap())
    decoder_layer(nc, *args)
    r = _run(nc, [arrays], core_ids=[0])
    return r.results[0]["out_x"]
```

```python
import concourse.bass as bass
from concourse import mybir
from contextlib import ExitStack


def decoder_layer(
    nc: bass.Bass,
    x_in: bass.AP,
    ctx_in: bass.AP,
    attn_Wq: bass.AP,
    attn_bq: bass.AP,
    attn_Wo: bass.AP,
    attn_M: bass.AP,
    attn_z: bass.AP,
    x_Wq: bass.AP,
    x_Wk: bass.AP,
    x_Wv: bass.AP,
    x_Wo: bass.AP,
    router_w: bass.AP,
    router_b: bass.AP,
    expert_b: bass.AP,
    out: bass.AP,
):
    F = mybir.dt.float32
    R = mybir.dt.float32r
    ALU = mybir.AluOpType
    ACT = mybir.ActivationFunctionType
    AX = mybir.AxisListType.X

    P = 128
    B, S, D = x_in.shape
    NT = B * S // P
    KC = D // P
    NTOK = B * S
    HALF = NTOK // 2
    H = attn_Wq.shape[0] // P
    MH = attn_M.shape[0]
    GREP = H // MH
    KV = x_Wk.shape[1] // P
    GH = H // KV
    NE = router_w.shape[0]
    SCALE = float(P) ** -0.5
    LN_EPS = 1e-5
    DEN_EPS = 1e-6
    assert (NT, KC, H, MH, KV, GH, NE) == (8, 4, 32, 8, 4, 8, 64)

    x_tiles = x_in.rearrange("b s d -> (b s) d").rearrange("(t p) d -> p t d", p=P)
    ctx_tiles = ctx_in.rearrange("b s d -> (b s) d").rearrange("(t p) d -> p t d", p=P)
    out_tiles = out.rearrange("b s d -> (b s) d").rearrange("(t p) d -> p t d", p=P)
    wqa_heads = attn_Wq.rearrange("(m g p) k -> g p m k", g=GREP, p=P)[0]
    bq_rows = attn_bq.rearrange("(m g p) -> g m p", g=GREP, p=P)[0]
    woa_heads = attn_Wo.rearrange("(o p) (m c) -> m p o c", p=P, m=MH)
    mem_heads = attn_M.rearrange("m d e -> d m e")
    wk_rows = x_Wk.rearrange("(k p) n -> p k n", p=P)
    wv_rows = x_Wv.rearrange("(k p) n -> p k n", p=P)
    wq_rows = x_Wq.rearrange("(k p) n -> p k n", p=P)
    wo_rows = x_Wo.rearrange("(h p) n -> p h n", p=P)

    keys_dram = nc.dram_tensor("keys_dram", (KV, 2, P, NTOK), F, kind="Internal").ap()
    vals_dram = nc.dram_tensor("vals_dram", (2, NTOK, KV * P), F, kind="Internal").ap()

    ctx = ExitStack()
    with ctx:
        def sb(name, shape, dt=F, stack=ctx):
            return stack.enter_context(nc.sbuf_tensor(name, shape, dt))

        def sem(name):
            return ctx.enter_context(nc.semaphore(name))

        resid = sb("resid", [P, NT, D])
        xnT = sb("xnT", [P, 2, KC, NTOK], R)
        regA = sb("regA", [P, 2, 4096], R)
        regC = sb("regC", [P, 2, 4096], R)
        raw16 = sb("raw16", [P, 4096])
        ident = sb("ident", [P, P])
        neg_half = sb("neg_half", [P, 1])
        bz = sb("bz", [P, 2 * MH])
        neg_bq = sb("neg_bq", [P, MH])
        rden = sb("rden", [P, 2, 4])
        stats = sb("stats", [P, 6])
        meanvar = sb("meanvar", [P, 2])
        vareps = sb("vareps", [P, 1])
        rstd = sb("rstd", [P, 1])
        negmax = sb("negmax", [P, 2, 4])
        rowsum = sb("rowsum", [P, 2, 4])
        rrow = sb("rrow", [P, 2, 4])

        first = ExitStack()
        regB = sb("regB", [P, 2, 4096], R, first)
        rawk = sb("rawk", [P, 4096], F, first)
        sig = sb("sig", [P, 3, HALF], F, first)
        qneg = sb("qneg", [P, HALF], F, first)
        qpos = sb("qpos", [P, HALF], F, first)
        wofold = sb("wofold", [P, 2, KC, P], F, first)
        wofT = sb("wofT", [P, 2, D], R, first)
        memT = sb("memT", [P, 2, P], R, first)
        mem = sb("mem", [P, MH // 2, P], F, first)
        xn = sb("xn", [P, 2, D], F, first)
        kvout = sb("kvout", [P, 2, D], F, first)
        first.close()

        second = ExitStack()
        qT = sb("qT", [P, 2, 8, GH, S], F, second)
        oT = sb("oT", [P, 2, 2, GH, P], R, second)
        wq_raw = sb("wq_raw", [P, KC, 2 * P], F, second)
        k_ring = sb("k_ring", [P, 4, 2, P], F, second)
        v_raw = sb("v_raw", [P, 2, 2, P], F, second)
        v_ring = sb("v_ring", [P, 2, 2, 2, P], R, second)
        probs = sb("probs", [P, 2, 4, P], F, second)
        pT = sb("pT", [P, 2, 2, 4 * P], R, second)
        second.close()
        bank = [ctx.enter_context(nc.psum_tensor(f"bank{i}", [P, 512], F)) for i in range(8)]

        ctxT = regA[:, :, :].rearrange("p a (k n) -> p a k n", k=KC)
        sigT = regA[:, :, :].rearrange("p a (m n) -> p a m n", m=MH)
        wq = regA[:, :, :].rearrange("p a (h k n) -> p a h k n", h=GH, k=KC)
        wkv1 = regB[:, :, :].rearrange("p a (w k n) -> p a w k n", w=2, k=KC)
        memwo = regB[:, :, :].rearrange("p a (m n) -> p a m n", m=MH)
        wqaT = regC[:, :, :].rearrange("p a (m k n) -> p a m k n", m=MH, k=KC)
        wkv2 = regC[:, :, :].rearrange("p a (w k n) -> p a w k n", w=2, k=KC)
        wo = regC[:, :, :].rearrange("p a (h n) -> p a h n", h=GH)
        ctx_raw = raw16[:, :].rearrange("p (t n) -> p t n", t=NT)
        woa_raw = raw16[:, :].rearrange("p (r o g n) -> p r o g n", r=2, o=KC, g=GREP)
        wo_raw = raw16[:, :].rearrange("p (h n) -> p h n", h=GH)
        wkv_raw = rawk[:, :].rearrange("p (w k n) -> p w k n", w=2, k=KC)
        wqa_raw = rawk[:, :].rearrange("p (m n) -> p m n", m=MH)
        bz_rows = sig[0:2 * MH, 0, 0:P]
        kv_slots = (qneg[:, :], qpos[:, :], kvout[:, 0, :], kvout[:, 1, :])
        e_xn = raw16[:, 0:2 * D].rearrange("p (r n) -> p r n", r=2)
        e_xnT = raw16[:, 2 * D:4 * D].rearrange("p (r k n) -> p r k n", r=2, k=KC)
        e_out = raw16[:, 4 * D:6 * D].rearrange("p (r n) -> p r n", r=2)

        def e_xn_of(e):
            return probs[:, 0, :, :].rearrange("p c n -> p (c n)") if e == NT - 1 else e_xn[:, e % 2, :]

        def e_out_of(e):
            return probs[:, 1, :, :].rearrange("p c n -> p (c n)") if e == NT - 1 else e_out[:, e % 2, :]

        rout_rows = raw16[0:NE, 5 * D:6 * D]
        expert = raw16[0:NE, 6 * D:7 * D]
        routT = raw16[:, 7 * D:7 * D + KC * NE].rearrange("p (k n) -> p k n", k=KC)
        wq_flat = wq_raw[:, :, :].rearrange("p k n -> p (k n)")
        small = wq_flat[:, 0:10 * NE].rearrange("p (r w n) -> p r w n", r=2, w=5)
        e_wT = wq_flat[0:NE, 10 * NE:10 * NE + 2 * P].rearrange("p (r n) -> p r n", r=2)
        rout_b = wq_flat[:, 14 * NE:15 * NE]
        top = wq_flat[:, 15 * NE:16 * NE].rearrange("p (r w n) -> p r w n", r=2, w=4)

        ctx_loaded = [sem(f"ctx_loaded{i}") for i in range(5)]
        wkv_loaded = [[sem(f"wv_loaded{i}") for i in range(2)], [sem(f"wk_loaded{i}") for i in range(2)]]
        x_loaded = [sem(f"x_loaded{i}") for i in range(4)]
        bz_loaded = sem("bz_loaded")
        mem_loaded = sem("mem_loaded")
        wqa_loaded = [sem(f"wqa_loaded{i}") for i in range(4)]
        woa_loaded = [sem(f"woa_loaded{i}") for i in range(2)]
        expert_loaded = sem("expert_loaded")
        consts_set = sem("consts_set")
        tr_done = sem("tr_done")
        tr_hi = sem("tr_hi")
        tr_used = sem("tr_used")
        mm_done = sem("mm_done")
        mm_act = sem("mm_act")
        mm_dve = sem("mm_dve")
        wkv_hi = sem("wkv_hi")
        wkv_lo = sem("wkv_lo")
        kv_written = [sem(f"kv_written{i}") for i in range(4)]
        dve_step = sem("dve_step")
        var_ready = sem("var_ready")
        rstd_ready = sem("rstd_ready")
        xn_ready = sem("xn_ready")
        qneg_ready = sem("qneg_ready")
        qexp_ready = sem("qexp_ready")
        sig_ready = sem("sig_ready")
        sig_scaled = sem("sig_scaled")
        sig_hi = sem("sig_hi")
        sig_lo = sem("sig_lo")
        spread_done = sem("spread_done")
        den_done = sem("den_done")
        rden_ready = sem("rden_ready")
        fold_half = sem("fold_half")
        fold_done = sem("fold_done")
        y_done = sem("y_done")
        y_used = sem("y_used")
        k_loaded = [sem(f"k_loaded{i}") for i in range(4)]
        v_loaded = [sem(f"v_loaded{i}") for i in range(2)]
        wq_loaded = sem("wq_loaded")
        wo_loaded = sem("wo_loaded")
        wq_hi = sem("wq_hi")
        wq_lo = sem("wq_lo")
        wo_hi = sem("wo_hi")
        wo_lo = sem("wo_lo")
        wo_used = sem("wo_used")
        v_hi = sem("v_hi")
        v_lo = sem("v_lo")
        q_done = sem("q_done")
        q_saved = sem("q_saved")
        scores_done = sem("scores_done")
        negmax_ready = sem("negmax_ready")
        rrow_ready = sem("rrow_ready")
        exp_done = sem("exp_done")
        probs_ready = sem("probs_ready")
        pT_done = sem("pT_done")
        pT_hi = sem("pT_hi")
        pT_lo = sem("pT_lo")
        pv_done = sem("pv_done")
        oT_hi = sem("oT_hi")
        oT_lo = sem("oT_lo")
        proj_done = sem("proj_done")
        proj_added = sem("proj_added")
        routT_done = sem("routT_done")
        routT_ready = sem("routT_ready")
        e_xn_ready = sem("e_xn_ready")
        e_tr_done = sem("e_tr_done")
        e_xnT_ready = sem("e_xnT_ready")
        logits_done = sem("logits_done")
        logits_saved = sem("logits_saved")
        e_max_ready = sem("e_max_ready")
        e_exp_done = sem("e_exp_done")
        e_w_ready = sem("e_w_ready")
        e_wT_done = sem("e_wT_done")
        e_wT_ready = sem("e_wT_ready")
        mix_done = sem("mix_done")
        e_scaled = sem("e_scaled")
        e_out_ready = sem("e_out_ready")
        out_written = [sem("out_written0"), sem("out_written1")]

        TR_CTX, TR_BZ, TR_X, TR_MEM, TR_X2 = 0, 8, 9, 25, 41
        MM_VCTX, MM_KCTX, MM_MEM, MM_VLAT, MM_KLAT, MM_XQ = 0, 8, 16, 40, 48, 56

        def tr_x(t):
            return TR_X + t if t < 2 else TR_X + 2 * (t - 1)

        def tr_wqa(m):
            return tr_x(m + 2) + 1 if m < MH - 2 else tr_x(NT - 1) + m - (MH - 4)

        def tr_mem(m):
            return TR_MEM + 2 * m

        def mm_query(i):
            return MM_MEM + (max(2 * i - 1, 0) if i <= MH else MH + i)

        def mm_memwo(m):
            return MM_MEM + 2 * m + 2

        def tr_hi_count(k):
            return k + 1 - (k >= TR_BZ)

        def mm_dve_count(k):
            return min(max((k - MM_MEM) // 2, 0), MH)

        def tr_bank(k):
            return bank[k % 2]

        def mm_bank(k):
            return bank[2 + k % 2]

        den_bank = bank[4]

        def spread_bank(i):
            return bank[5 + i % 2]

        def e_banks(e):
            return {0: (1, 0), NT - 2: (1, 0), NT - 1: (3, 2)}.get(e, (6, 6))

        def y_bank(t):
            return bank[4] if t % 2 else bank[7]

        PARTS = ((0, 0), (0, 1), (1, 0))

        block = ctx.enter_context(nc.Block())

        @block.sync
        def _(sp):
            def load_ctx(i):
                sp.dma_start(ctx_raw[:, 2 * i:2 * i + 2, :], ctx_tiles[:, 2 * i:2 * i + 2, :])\
                  .then_inc(ctx_loaded[i], 16)

            def load_wkv(w, halves=(0, 1)):
                for i in halves:
                    sp.dma_start(wkv_raw[:, w, 2 * i:2 * i + 2, :], (wv_rows, wk_rows)[w][:, 2 * i:2 * i + 2, :])\
                      .then_inc(wkv_loaded[w][i], 16)

            sp.dma_start(ctx_raw[:, 0, :], ctx_tiles[:, 0, :]).then_inc(ctx_loaded[0], 16)
            load_wkv(0, (0,))
            sp.dma_start(ctx_raw[:, 1, :], ctx_tiles[:, 1, :]).then_inc(ctx_loaded[4], 16)
            load_wkv(0, (1,))
            for i in range(1, 4):
                load_ctx(i)
            load_wkv(1)
            for i in range(4):
                sp.dma_start(resid[:, 2 * i:2 * i + 2, :], x_tiles[:, 2 * i:2 * i + 2, :])\
                  .then_inc(x_loaded[i], 16)
            sp.dma_start(bz_rows[0:MH, :], bq_rows).then_inc(bz_loaded, 16)
            sp.dma_start(bz_rows[MH:2 * MH, :], attn_z).then_inc(bz_loaded, 16)
            sp.dma_start(mem[:, :, :], mem_heads[:, 0:MH // 2, :]).then_inc(mem_loaded, 16)
            for i in range(4):
                if i % 2 == 0:
                    sp.wait_ge(wkv_lo, 2 * i + KC)
                sp.dma_start(wqa_raw[:, 2 * i:2 * i + 2, :], wqa_heads[:, 2 * i:2 * i + 2, :])\
                  .then_inc(wqa_loaded[i], 16)
            sp.wait_ge(tr_done, TR_CTX + NT)
            for m in range(MH):
                if m >= 2:
                    sp.wait_ge(fold_done, m - 1)
                sp.dma_start(woa_raw[:, m % 2, :, :, :].rearrange("p o g n -> p o (g n)"),
                             woa_heads[m]).then_inc(woa_loaded[m % 2], 16)
                if m == 6:
                    sp.wait_ge(tr_done, tr_mem(3) + 1)
                    sp.dma_start(mem[:, :, :], mem_heads[:, MH // 2:MH, :]).then_inc(mem_loaded, 16)
            sp.wait_ge(tr_done, tr_wqa(MH - 1) + 1)
            for w in range(2):
                load_wkv(w)
            sp.wait_ge(fold_done, MH)
            sp.dma_start(wo_raw, wo_rows[:, 0:GH, :]).then_inc(wo_loaded, 16)
            sp.wait_ge(sig_lo, 2 * MH)
            for j in range(4):
                if j:
                    sp.wait_ge(wq_lo, j)
                sp.dma_start(wq_raw[:, :, :], wq_rows[:, :, 2 * j * P:(2 * j + 2) * P]).then_inc(wq_loaded, 16)
            for r in range(4):
                sp.wait_ge(kv_written[r], 16 * 8)

            def load_k(g, t):
                sp.dma_start(k_ring[:, t % 4, :, :],
                             keys_dram[bass.ds(g, 1), :, :, t * P:(t + 1) * P].rearrange("g s d n -> d (g s) n"))\
                  .then_inc(k_loaded[t % 4], 16)

            def load_v(g, t):
                for s in range(2):
                    sp.dma_start(v_raw[s * S:(s + 1) * S, t % 2, :, :],
                                 vals_dram[s, t * P:(t + 1) * P, bass.ds(g * P, P)]
                                 .rearrange("(b s) n -> s b n", b=2)).then_inc(v_loaded[t % 2], 16)

            for t in range(3):
                load_k(0, t)
            for t in range(2):
                load_v(0, t)

            def step(g, t, last, first_step=False):
                n = 8 * g + t
                if not (last and t >= 5):
                    if not first_step:
                        sp.wait_ge(scores_done, 2 * n)
                    load_k(g + (t + 3) // 8, (t + 3) % 8)
                if not (last and t >= 6):
                    sp.wait_ge(v_lo, n + 1)
                    load_v(g + (t + 2) // 8, (t + 2) % 8)
                if last:
                    return
                if t == 1:
                    sp.wait_ge(wo_lo, 8 * g + 8)
                    sp.dma_start(wo_raw, wo_rows[:, bass.ds(8 * g + 8, GH), :]).then_inc(wo_loaded, 16)
                if 1 <= t <= 4:
                    j = t - 1
                    sp.wait_ge(wq_lo, 4 * g + 4 + j)
                    sp.dma_start(wq_raw[:, :, :],
                                 wq_rows[:, :, bass.ds((g + 1) * (GH * P) + 2 * j * P, 2 * P)])\
                      .then_inc(wq_loaded, 16)

            step(0, 0, False, True)
            with sp.Fori(0, KV - 1) as g:
                for t in range(1, NT):
                    step(g, t, False)
                step(g + 1, 0, False)
            def store(t):
                sp.wait_ge(e_out_ready, t + 1)
                sp.dma_start(out_tiles[:, t, :], e_out_of(t)).then_inc(out_written[t % 2], 16)

            for t in range(1, NT):
                step(KV - 1, t, True)
                if t >= 3:
                    store(t - 3)
                if t == 1:
                    sp.wait_ge(wo_lo, KV * GH)
                    sp.dma_start(rout_rows, router_w).then_inc(expert_loaded, 16)
                    sp.dma_start(rout_b, router_b.rearrange("(a n) -> a n", a=1).broadcast_to([P, NE]))\
                      .then_inc(expert_loaded, 16)
                    sp.dma_start(expert, expert_b).then_inc(expert_loaded, 16)
            for t in range(NT - 3, NT):
                store(t)
            for r in range(2):
                sp.wait_ge(out_written[r], 16 * NT // 2)

        @block.gpsimd
        def _(pool):
            nc.gpsimd.memset(neg_half[:, :], -0.5).then_inc(consts_set, 1)
            nc.gpsimd.memset(ident[:, :], 0.0).then_inc(consts_set, 1)
            pool.wait_ge(consts_set, 2)
            nc.gpsimd.affine_select(out=ident[:, :], in_=ident[:, :], compare_op=ALU.not_equal, fill=1.0,
                                    base=0, pattern=[[-1, P]], channel_multiplier=1).then_inc(consts_set, 1)

            def root(k):
                pool.wait_ge(var_ready, k + 1)
                nc.gpsimd.tensor_tensor(rstd[:, :], vareps[:, :], neg_half[:, :], ALU.pow)\
                    .then_inc(rstd_ready, 1)

            for t in range(NT):
                root(t)
            for m in range(MH):
                pool.wait_ge(woa_loaded[m % 2], 16 * (m // 2 + 1))
                w = woa_raw[:, m % 2, :, :, :]
                nc.gpsimd.tensor_tensor(w[:, :, 0:2, :], w[:, :, 0:2, :], w[:, :, 2:4, :], ALU.add)\
                    .then_inc(fold_half, 1)
                pool.wait_ge(fold_half, m + 1)
                if m >= 2:
                    pool.wait_ge(tr_done, tr_mem(m - 2) + 2)
                nc.gpsimd.tensor_tensor(wofold[:, m % 2, :, :], w[:, :, 0, :], w[:, :, 1, :], ALU.add)\
                    .then_inc(fold_done, 1)
            for k in range(NT, 3 * NT):
                root(k)

        @block.tensor
        def _(pe):
            pe.wait_ge(consts_set, 3)

            def tr_free(k):
                if k >= 2:
                    pe.wait_ge(tr_used, k - 1)

            def mm_free(k):
                if k >= 2:
                    pe.wait_ge(mm_act, k - 1)
                    if mm_dve_count(k - 2):
                        pe.wait_ge(mm_dve, mm_dve_count(k - 2))

            def transpose_rows(k, rows):
                tr_free(k)
                for c in range(KC):
                    last = nc.tensor.transpose(tr_bank(k)[:, c * P:(c + 1) * P],
                                               rows[:, c * P:(c + 1) * P], ident[:, :])
                last.then_inc(tr_done, 1)

            def product(k, left, right):
                mm_free(k)
                terms = [(a, b, c) for c in range(KC) for a, b in PARTS]
                for i, (a, b, c) in enumerate(terms):
                    last = nc.tensor.matmul(mm_bank(k)[:, :], left(a, c), right(b, c),
                                            start=i == 0, stop=i == len(terms) - 1)
                last.then_inc(mm_done, 1)

            def context_transposes(i, tiles=None):
                pe.wait_ge(ctx_loaded[i], 16)
                for t in tiles or (2 * i, 2 * i + 1):
                    transpose_rows(TR_CTX + t, ctx_raw[:, t, :])

            def keys(k, wkv, srcT, half, g):
                product(k,
                            lambda a, c: wkv[:, a, 1, c, g * P:(g + 1) * P],
                            lambda b, c: srcT[:, b, c, half * HALF:(half + 1) * HALF])

            def values(k, wkv, srcT, t):
                product(k, lambda a, c: srcT[:, a, c, t * P:(t + 1) * P],
                        lambda b, c: wkv[:, b, 0, c, :])

            context_transposes(0, (0,))
            for t, c in ((0, 0), (0, 1), (1, 0), (1, 1), (0, 2), (1, 2), (0, 3), (1, 3)):
                if (t, c) == (1, 0):
                    context_transposes(4, (1,))
                if (t, c) == (0, 3):
                    context_transposes(1)
                pe.wait_ge(tr_used, TR_CTX + t + 1)
                pe.wait_ge(wkv_lo, c + 1)
                for i, (a, b) in enumerate(PARTS):
                    last = nc.tensor.matmul(mm_bank(MM_VCTX + t)[:, :], ctxT[:, a, c, t * P:(t + 1) * P],
                                            wkv1[:, b, 0, c, :], start=c == 0 and i == 0,
                                            stop=c == KC - 1 and i == 2)
                if c == KC - 1:
                    last.then_inc(mm_done, 1)
            for t in range(2, NT):
                pe.wait_ge(tr_used, TR_CTX + t + 1)
                values(MM_VCTX + t, wkv1, ctxT, t)
                if t < 4:
                    context_transposes(t)

            def memory_wq(m):
                if m % 2 == 0:
                    pe.wait_ge(wqa_loaded[m // 2], 16)
                transpose_rows(tr_wqa(m), wqa_raw[:, m, :])

            def x_transposes(t):
                pe.wait_ge(xn_ready, t + 1)
                transpose_rows(tr_x(t), xn[:, t % 2, :])

            pe.wait_ge(bz_loaded, 32)
            tr_free(TR_BZ)
            nc.tensor.transpose(tr_bank(TR_BZ)[:, 0:2 * MH], bz_rows, ident[0:2 * MH, 0:2 * MH])\
                .then_inc(tr_done, 1)
            x_transposes(0)
            pe.wait_ge(wkv_lo, 2 * KC)
            for i in range(NT):
                if i + 1 < NT:
                    x_transposes(i + 1)
                if i:
                    memory_wq(i - 1)
                if i == NT - 1:
                    memory_wq(i)
                keys(MM_KCTX + i, wkv1, ctxT, i // KV, i % KV)

            def memory_query(i):
                half, m = divmod(i, MH)
                if half == 0:
                    pe.wait_ge(tr_used, tr_wqa(m) + 1)
                product(mm_query(i),
                        lambda a, c: wqaT[:, a, m, c, :],
                        lambda b, c: xnT[:, b, c, half * HALF:(half + 1) * HALF])

            def denominators(i):
                pe.wait_ge(sig_ready, i + 1)
                if i:
                    pe.wait_ge(rden_ready, i)
                if i == MH + 1:
                    pe.wait_ge(y_used, 4)
                for tt in range(4):
                    last = nc.tensor.matmul(den_bank[:, tt:tt + 1], sig[:, i % 3, tt * P:(tt + 1) * P],
                                            bz[:, MH + i % MH:MH + i % MH + 1], start=True, stop=True)
                last.then_inc(den_done, 1)

            def spread(i):
                pe.wait_ge(rden_ready, i + 1)
                if i >= 2:
                    pe.wait_ge(sig_scaled, i - 1)
                for tt in range(4):
                    last = nc.tensor.transpose(spread_bank(i)[:, tt * P:(tt + 1) * P],
                                               rden[:, i % 2, tt:tt + 1].broadcast_to([P, P]), ident[:, :])
                last.then_inc(spread_done, 1)

            def memory_transposes(m):
                k = tr_mem(m)
                if m % 4 == 0:
                    pe.wait_ge(mem_loaded, 16 * (m // 4 + 1))
                tr_free(k)
                nc.tensor.transpose(tr_bank(k)[:, 0:P], mem[:, m % 4, :], ident[:, :]).then_inc(tr_done, 1)

            def wo_transposes(m):
                k = tr_mem(m) + 1
                pe.wait_ge(fold_done, m + 1)
                tr_free(k)
                for c in range(KC):
                    last = nc.tensor.transpose(tr_bank(k)[:, c * P:(c + 1) * P],
                                               wofold[:, m % 2, c, :], ident[:, :])
                last.then_inc(tr_done, 1)

            def memory_weights(m):
                k = mm_memwo(m)
                mm_free(k)
                pe.wait_ge(tr_used, tr_mem(m) + 2)
                for i, (a, b) in enumerate(PARTS):
                    last = nc.tensor.matmul(mm_bank(k)[:, :], memT[:, a, :], wofT[:, b, :],
                                            start=i == 0, stop=i == 2)
                last.then_inc(mm_done, 1)

            def memory_head(i):
                memory_query(i)
                if i:
                    denominators(i - 1)
                if 1 <= i <= MH:
                    memory_weights(i - 1)
                if i < MH:
                    memory_transposes(i)
                if i >= 2:
                    spread(i - 2)
                if i < MH:
                    wo_transposes(i)

            def memory_output(t, heads=range(MH)):
                for m in heads:
                    if m == 0 and t >= 2:
                        pe.wait_ge(y_used, t - 1)
                    if t % 4 == 0:
                        pe.wait_ge(sig_lo, t // 4 * MH + m + 1)
                    if t == 0:
                        pe.wait_ge(mm_dve, mm_dve_count(mm_memwo(m)))
                    for i, (a, b) in enumerate(PARTS):
                        last = nc.tensor.matmul(y_bank(t)[:, :],
                                                sigT[:, a, m, (t % 4) * P:(t % 4 + 1) * P],
                                                memwo[:, b, m, :], start=m == 0 and i == 0,
                                                stop=m == MH - 1 and i == 2)
                if heads[-1] == MH - 1:
                    last.then_inc(y_done, 1)

            def latent_transposes(t):
                pe.wait_ge(xn_ready, NT + t + 1)
                transpose_rows(TR_X2 + t, xn[:, t % 2, :])

            for i in range(MH + 2):
                memory_head(i)
            memory_output(0)
            pe.wait_ge(rden_ready, MH + 1)
            for t in range(1, 4):
                memory_output(t)
                latent_transposes(t - 1)
            for i in range(MH + 2, 2 * MH):
                memory_head(i)
                if i == MH + 3:
                    latent_transposes(3)
            memory_output(4, range(0, 5))
            denominators(2 * MH - 1)
            spread(2 * MH - 2)
            memory_output(4, range(5, 6))
            spread(2 * MH - 1)
            for m in range(4):
                pe.wait_ge(sig_lo, MH + m + 1)
            memory_output(5, range(0, 4))
            memory_output(4, range(6, MH))
            memory_output(5, range(4, MH))
            for t in range(6, NT):
                memory_output(t)
                latent_transposes(t - 2)
            pe.wait_ge(wkv_lo, 3 * KC)
            for t in range(4):
                values(MM_VLAT + t, wkv2, xnT, t)
                if t in (0, 3):
                    latent_transposes(6 + t // 3)
            for t in range(4, NT):
                pe.wait_ge(tr_used, TR_X2 + t + 1)
                values(MM_VLAT + t, wkv2, xnT, t)
            pe.wait_ge(wkv_lo, 4 * KC)
            for i in range(NT):
                keys(MM_KLAT + i, wkv2, xnT, i // KV, i % KV)

            def queries(k_bank, head, half, done):
                for i, (c, (a, b)) in enumerate((c, ab) for c in range(KC) for ab in PARTS):
                    last = nc.tensor.matmul(k_bank[:, :], wq[:, a, head, c, :],
                                            xnT[:, b, c, half * HALF:(half + 1) * HALF],
                                            start=i == 0, stop=i == 3 * KC - 1)
                last.then_inc(done, 1)

            for h in range(GH):
                k = MM_XQ + h
                mm_free(k)
                if h % 2 == 0:
                    pe.wait_ge(wq_lo, h // 2 + 1)
                queries(mm_bank(k), h, 0, mm_done)

            def project(g, t, parity, release):
                n = 8 * g + t
                pe.wait_ge(oT_lo, 2 * n + 2)
                pe.wait_ge(proj_added, n + 1)
                for h in range(GH):
                    if t == 0:
                        pe.wait_ge(wo_lo, 8 * g + h + 1)
                    for i, (a, b) in enumerate(PARTS):
                        last = nc.tensor.matmul(bank[7][:, :], oT[:, parity, a, h, :], wo[:, b, h, :],
                                                start=h == 0 and i == 0, stop=h == GH - 1 and i == 2)
                    if release and h < GH - 1:
                        last.then_inc(wo_used, 1)
                last.then_inc(proj_done, 1)

            attended = 2 * KV * NT
            QUERIES = 2 * KV * GH - GH

            def router_transposes(t):
                pe.wait_ge(expert_loaded, 48)
                pe.wait_ge(oT_lo, 2 * (8 * (KV - 1) + t))
                for c in range(KC):
                    last = nc.tensor.transpose(bank[5][:, c * NE:(c + 1) * NE],
                                               rout_rows[:, c * P:(c + 1) * P], ident[0:NE, 0:NE])
                last.then_inc(routT_done, 1)

            def expert_transposes(e):
                pe.wait_ge(e_xn_ready, e + 1)
                pe.wait_ge(oT_lo, min(2 * (8 * (KV - 1) + e + 2) - 1, attended))
                if e:
                    pe.wait_ge(e_xnT_ready, e)
                for c in range(KC):
                    last = nc.tensor.transpose(bank[4][:, c * P:(c + 1) * P],
                                               e_xn_of(e)[:, c * P:(c + 1) * P], ident[:, :])
                last.then_inc(e_tr_done, 1)

            def expert_logits(e):
                pe.wait_ge(e_xnT_ready, e + 1)
                pe.wait_ge(oT_lo, min(2 * (8 * (KV - 1) + e + 2), attended))
                if e:
                    pe.wait_ge(logits_saved, e)
                for c in range(KC):
                    last = nc.tensor.matmul(bank[5][:, 0:NE], e_xnT[:, e % 2, c, :], routT[:, c, :],
                                            start=c == 0, stop=c == KC - 1)
                last.then_inc(logits_done, 1)

            def expert_weights(e):
                pe.wait_ge(e_w_ready, e + 1)
                if e in (0, NT - 2):
                    pe.wait_ge(exp_done, min(2 * (8 * (KV - 1) + e + 3) + 2, attended))
                elif e == NT - 1:
                    pe.wait_ge(pT_lo, attended)
                elif e == 1:
                    pe.wait_ge(q_saved, QUERIES)
                else:
                    pe.wait_ge(e_out_ready, e)
                nc.tensor.transpose(bank[e_banks(e)[0]][0:NE, 0:P], small[:, e % 2, 4, :], ident[:, :])\
                    .then_inc(e_wT_done, 1)

            def expert_mix(e):
                pe.wait_ge(e_wT_ready, e + 1)
                nc.tensor.matmul(bank[e_banks(e)[1]][:, :], e_wT[:, e % 2, :], expert[:, :], start=True, stop=True)\
                    .then_inc(mix_done, 1)

            def step(g, t, last_group, first_step=False):
                n = 8 * g + t
                half = t // 4
                if first_step:
                    pe.wait_ge(mm_act, MM_XQ + GH)
                    pe.wait_ge(tr_used, TR_X2 + NT)
                elif t % 4 == 0:
                    pe.wait_ge(q_saved, 16 * g + 2 * t)
                pe.wait_ge(k_loaded[t % 4], 16 * (2 * g + half + 1))
                for bb in range(2):
                    if last_group and t == 4:
                        pe.wait_ge((e_out_ready, e_wT_ready)[bb], 1)
                    if not first_step:
                        pe.wait_ge(exp_done, 2 * n - 1 + bb)
                    for p in range(4):
                        last = nc.tensor.matmul(bank[bb][:, p * P:(p + 1) * P],
                                                qT[:, half, (2 * t + bb) % 8, 2 * p:2 * p + 2, :]
                                                .rearrange("p h s -> p (h s)"),
                                                k_ring[:, t % 4, :, bb * S:(bb + 1) * S],
                                                start=True, stop=True)
                    last.then_inc(scores_done, 1)

                def next_queries(u):
                    if last_group and t >= 4:
                        return
                    k = 16 * g + 2 * t + u
                    if first_step and u == 0:
                        pe.wait_ge(sig_scaled, 2 * MH)
                    else:
                        pe.wait_ge(q_saved, k)
                    head = 2 * (t % 4) + u
                    if t >= 4 and u == 0:
                        pe.wait_ge(wq_lo, 4 * g + 4 + t - 3)
                    queries(bank[6], head, 1 - half, q_done)

                next_queries(0)
                if not first_step:
                    if t == 0:
                        project(g - 1, 7, 1, True)
                    else:
                        project(g, t - 1, (t - 1) % 2, False)
                if last_group and t >= 2:
                    expert_transposes(t - 2)
                if last_group and t >= 3:
                    expert_weights(t - 3)
                for bb in range(2):
                    pe.wait_ge(probs_ready, 2 * n + bb + 1)
                    if not first_step:
                        pe.wait_ge(pT_lo, 2 * n - 1 + bb)
                    for p in range(4):
                        last = nc.tensor.transpose(bank[2 + bb][:, p * P:(p + 1) * P],
                                                   probs[:, bb, p, :], ident[:, :])
                    last.then_inc(pT_done, 1)
                if last_group and t == 1:
                    router_transposes(t)
                if last_group and t >= 2:
                    expert_logits(t - 2)
                if last_group and t >= 3:
                    expert_mix(t - 3)
                next_queries(1)
                pe.wait_ge(v_lo, n + 1)
                for bb in range(2):
                    pe.wait_ge(pT_lo, 2 * n + bb + 1)
                    if first_step:
                        pe.wait_ge(y_used, NT)
                    else:
                        pe.wait_ge(oT_lo, 2 * n - 1 + bb)
                    if last_group and t == 1 and bb == 1:
                        pe.wait_ge(routT_ready, 1)
                    if last_group and t >= 2:
                        pe.wait_ge((e_xnT_ready, logits_saved)[bb], t - 1)
                    for i, (a, b) in enumerate(PARTS):
                        last = nc.tensor.matmul(bank[4 + bb][:, :], v_ring[:, t % 2, bb, a, :],
                                                pT[:, bb, b, :], start=i == 0, stop=i == 2)
                    last.then_inc(pv_done, 1)

            step(0, 0, False, True)
            with pe.Fori(0, KV - 1) as g:
                for t in range(1, NT):
                    step(g, t, False)
                step(g + 1, 0, False)
            for t in range(1, NT):
                step(KV - 1, t, True)
            project(KV - 1, NT - 1, 1, False)
            expert_transposes(NT - 2)
            expert_weights(NT - 3)
            expert_mix(NT - 3)
            expert_logits(NT - 2)
            expert_transposes(NT - 1)
            expert_logits(NT - 1)
            for e in (NT - 2, NT - 1):
                expert_weights(e)
                expert_mix(e)

        @block.scalar
        def _(act):
            def high(dst, src):
                return nc.scalar.copy(dst, src)

            def wq_high(g, j):
                act.wait_ge(wq_loaded, 16 * (4 * g + j + 1))
                high(wq[:, 0, 2 * j:2 * j + 2, :, :],
                     wq_raw[:, :, :].rearrange("p k (h n) -> p h k n", h=2)).then_inc(wq_hi, 1)

            def v_high(g, t):
                act.wait_ge(v_loaded[t % 2], 32 * (4 * g + t // 2 + 1))
                high(v_ring[:, t % 2, :, 0, :], v_raw[:, t % 2, :, :]).then_inc(v_hi, 1)

            def wo_high(g, h):
                high(wo[:, 0, h, :], wo_raw[:, h, :]).then_inc(wo_hi, 1)

            def save_queries(k_bank, half, head, saved):
                nc.scalar.mul(qT[:, half, :, head, :], k_bank[:, :].rearrange("p (b s) -> p b s", b=8), SCALE)\
                    .then_inc(saved, 1)

            def tr_high(k, dst, src=None):
                act.wait_ge(tr_done, k + 1)
                high(dst, tr_bank(k)[:, :] if src is None else src).then_inc(tr_hi, 1)

            def blocks(k):
                return tr_bank(k)[:, :].rearrange("p (c n) -> p c n", c=KC)

            def wkv_high(w, wkv, loads, chunks=range(KC)):
                for c in chunks:
                    if c % 2 == 0:
                        act.wait_ge(wkv_loaded[w][c // 2], 16 * loads)
                    high(wkv[:, 0, w, c, :], wkv_raw[:, w, c, :]).then_inc(wkv_hi, 1)

            def ctx_high(t):
                tr_high(TR_CTX + t, ctxT[:, 0, :, t * P:(t + 1) * P], blocks(TR_CTX + t))

            def save_kv(k, n, dst):
                act.wait_ge(mm_done, k + 1)
                if n >= 4:
                    act.wait_ge(kv_written[n % 4], 16 * (n // 4))
                nc.scalar.copy(kv_slots[n % 4], mm_bank(k)[:, :]).then_inc(mm_act, 1)
                act.wait_ge(mm_act, k + 1)
                act.dma_start(dst, kv_slots[n % 4]).then_inc(kv_written[n % 4], 16)

            def save_key(k, n, s, i):
                g, half = i % KV, i // KV
                save_kv(k, n, keys_dram[g, s, :, half * HALF:(half + 1) * HALF])

            def save_value(t):
                save_kv(MM_VCTX + t, t, vals_dram[0, t * P:(t + 1) * P, :])

            ctx_high(0)
            wkv_high(0, wkv1, 1, (0, 1))
            ctx_high(1)
            wkv_high(0, wkv1, 1, (2, 3))
            ctx_high(2)
            ctx_high(3)
            save_value(0)
            save_value(1)
            for t in range(2, NT):
                if t < 4:
                    ctx_high(2 * t)
                    ctx_high(2 * t + 1)
                save_value(t)
                if t == 3:
                    wkv_high(1, wkv1, 1)

            def memory_wq(m):
                tr_high(tr_wqa(m), wqaT[:, 0, m, :, :], blocks(tr_wqa(m)))

            def x_high(t):
                tr_high(tr_x(t), xnT[:, 0, :, t * P:(t + 1) * P], blocks(tr_x(t)))

            x_high(0)
            for i in range(NT):
                if i + 1 < NT:
                    x_high(i + 1)
                if i:
                    memory_wq(i - 1)
                if i == NT - 1:
                    memory_wq(i)
                save_key(MM_KCTX + i, NT + i, 0, i)

            def memory_head(i):
                m = i % MH
                if i < 2 * MH:
                    k = mm_query(i)
                    act.wait_ge(mm_done, k + 1)
                    if i:
                        act.wait_ge(sig_ready, i)
                    nc.scalar.activation(qneg[:, :], mm_bank(k)[:, :], ACT.Relu, bias=neg_bq[:, m:m + 1],
                                         scale=-1.0).then_inc(qneg_ready, 1)
                    nc.scalar.activation(qpos[:, :], mm_bank(k)[:, :], ACT.Relu, bias=bz[:, m:m + 1])\
                        .then_inc(mm_act, 1)
                    act.wait_ge(qneg_ready, i + 1)
                    nc.scalar.activation(qneg[:, :], qneg[:, :], ACT.Exp, scale=-1.0).then_inc(qexp_ready, 1)
                if 1 <= i <= MH:
                    act.wait_ge(mm_done, mm_memwo(i - 1) + 1)
                    high(memwo[:, 0, i - 1, :], mm_bank(mm_memwo(i - 1))[:, :]).then_inc(mm_act, 1)
                if i < MH:
                    tr_high(tr_mem(i), memT[:, 0, :], tr_bank(tr_mem(i))[:, 0:P])
                    tr_high(tr_mem(i) + 1, wofT[:, 0, :])
                if i >= 2:
                    act.wait_ge(sig_scaled, i - 1)
                    high(sigT[:, 0, (i - 2) % MH, :], sig[:, (i - 2) % 3, :]).then_inc(sig_hi, 1)

            act.wait_ge(tr_used, TR_BZ + 1)
            for r in range(2):
                act.wait_ge(kv_written[r], 16 * 4)
            for i in range(MH + 2):
                memory_head(i)

            def latent_high(t):
                tr_high(TR_X2 + t, xnT[:, 0, :, t * P:(t + 1) * P], blocks(TR_X2 + t))

            for t in range(3):
                latent_high(t)
            act.wait_ge(y_done, 4)
            for i in range(MH + 2, 2 * MH + 2):
                memory_head(i)
                if i == MH + 3:
                    latent_high(3)
            for w in range(2):
                wkv_high(w, wkv2, 2)
                latent_high(4 + w)
            def save_latent_values(t):
                save_kv(MM_VLAT + t, 16 + t, vals_dram[1, t * P:(t + 1) * P, :])
                if t in (2, 5):
                    act.wait_ge(y_done, NT)
                    wq_high(0, t // 3)

            for t in range(4):
                save_latent_values(t)
                if t in (0, 3):
                    latent_high(6 + t // 3)
            for t in range(4, NT):
                save_latent_values(t)
            for half in range(2):
                for i in range(KV * half, KV * half + KV):
                    save_key(MM_KLAT + i, 24 + i, 1, i)
                wq_high(0, 2 + half)
            for h in range(GH):
                k = MM_XQ + h
                act.wait_ge(mm_done, k + 1)
                save_queries(mm_bank(k), 0, h, mm_act)
                if h == 0:
                    act.wait_ge(wo_loaded, 16)
                wo_high(0, h)
                if h == 5:
                    v_high(0, 0)

            def save_expert_xn(e):
                act.wait_ge(e_tr_done, e + 1)
                if e >= 2:
                    act.wait_ge(logits_done, e - 1)
                nc.scalar.copy(e_xnT[:, e % 2, :, :], bank[4][:, :].rearrange("p (k n) -> p k n", k=KC))\
                    .then_inc(e_xnT_ready, 1)

            def save_expert_weights(e):
                act.wait_ge(e_wT_done, e + 1)
                if e >= 2:
                    act.wait_ge(mix_done, e - 1)
                nc.scalar.copy(e_wT[:, e % 2, :], bank[e_banks(e)[0]][0:NE, 0:P]).then_inc(e_wT_ready, 1)

            def expert_exp(e):
                act.wait_ge(e_max_ready, e + 1)
                nc.scalar.activation(small[:, e % 2, 1, :], small[:, e % 2, 0, :], ACT.Exp,
                                     bias=top[:, e % 2, 1, 0:1], accum_out=top[:, e % 2, 2, 0:1])\
                    .then_inc(e_exp_done, 1)

            def step(g, t, last_group, first_step=False):
                n = 8 * g + t
                half = t // 4
                for bb in range(2):
                    act.wait_ge(negmax_ready, 2 * n + bb + 1)
                    if not first_step:
                        act.wait_ge(pT_done, 2 * n - 1 + bb)
                    for p in range(4):
                        last = nc.scalar.activation(probs[:, bb, p, :], bank[bb][:, p * P:(p + 1) * P], ACT.Exp,
                                                    bias=negmax[:, bb, p:p + 1],
                                                    accum_out=rowsum[:, bb, p:p + 1])
                    last.then_inc(exp_done, 1)

                def save_next(u):
                    if last_group and t >= 4:
                        return
                    act.wait_ge(q_done, 16 * g + 2 * t + u + 1)
                    save_queries(bank[6], 1 - half, 2 * (t % 4) + u, q_saved)

                save_next(0)
                if not (last_group and t == 7):
                    if not first_step:
                        act.wait_ge(pv_done, 2 * n)
                    v_high(g, t + 1)
                if not last_group and 2 <= t <= 5:
                    act.wait_ge(q_done, 16 * g + 2 * (t - 2) + 2)
                    wq_high(g + 1, t - 2)
                if t == 0 and not first_step:
                    act.wait_ge(wo_loaded, 16 * g + 16)
                    for h in range(GH):
                        if h < GH - 1:
                            act.wait_ge(wo_used, (GH - 1) * (g - 1) + h + 1)
                        else:
                            act.wait_ge(proj_done, 8 * g)
                        wo_high(g, h)
                if last_group and t >= 2:
                    save_expert_xn(t - 2)
                if last_group and t >= 3:
                    save_expert_weights(t - 3)
                for bb in range(2):
                    act.wait_ge(pT_done, 2 * n + bb + 1)
                    if not first_step:
                        act.wait_ge(pv_done, 2 * n - 1 + bb)
                    high(pT[:, bb, 0, :], bank[2 + bb][:, :]).then_inc(pT_hi, 1)
                save_next(1)
                for bb in range(2):
                    act.wait_ge(pv_done, 2 * n + bb + 1)
                    high(oT[:, t % 2, 0, :, bb * S:(bb + 1) * S],
                         bank[4 + bb][:, :].rearrange("p (h s) -> p h s", h=GH)).then_inc(oT_hi, 1)
                if last_group and t >= 2:
                    expert_exp(t - 2)

            step(0, 0, False, True)
            with act.Fori(0, KV - 1) as g:
                for t in range(1, NT):
                    step(g, t, False)
                step(g + 1, 0, False)
            for t in range(1, NT):
                step(KV - 1, t, True)

            save_expert_xn(NT - 2)
            save_expert_weights(NT - 3)
            save_expert_xn(NT - 1)
            expert_exp(NT - 2)
            save_expert_weights(NT - 2)
            expert_exp(NT - 1)
            save_expert_weights(NT - 1)

        @block.vector
        def _(dve):
            steps = [0]

            def settled(ins):
                steps[0] += 1
                ins.then_inc(dve_step, 1)
                dve.wait_ge(dve_step, steps[0])

            def low(dst, src, high):
                return nc.vector.tensor_tensor(dst, src, high.bitcast(F), ALU.subtract)

            def blocks(k):
                return tr_bank(k)[:, :].rearrange("p (c n) -> p c n", c=KC)

            def tr_low(k, dst, src, high):
                dve.wait_ge(tr_hi, tr_hi_count(k))
                low(dst, src, high).then_inc(tr_used, 1)

            def normalise(k, src, dst, done):
                settled(nc.vector.bn_stats(stats[:, :], src))
                settled(nc.vector.bn_aggr(meanvar[:, :], stats[:, :]))
                nc.vector.tensor_scalar(vareps[:, :], meanvar[:, 1:2], LN_EPS, None, ALU.add)\
                    .then_inc(var_ready, 1)
                dve.wait_ge(rstd_ready, k + 1)
                nc.vector.tensor_scalar(dst, src, meanvar[:, 0:1], rstd[:, 0:1],
                                        ALU.subtract, ALU.mult).then_inc(done, 1)

            def wkv_low(w, wkv, n, chunks=range(KC)):
                for c in chunks:
                    dve.wait_ge(wkv_hi, n + c + 1)
                    low(wkv[:, 1, w, c, :], wkv_raw[:, w, c, :], wkv[:, 0, w, c, :]).then_inc(wkv_lo, 1)

            for t in range(NT):
                cols = slice(t * P, (t + 1) * P)
                tr_low(TR_CTX + t, ctxT[:, 1, :, cols], blocks(TR_CTX + t), ctxT[:, 0, :, cols])
                if t < 2:
                    wkv_low(0, wkv1, 0, (2 * t, 2 * t + 1))
            wkv_low(1, wkv1, KC)

            def norm_x(t):
                if t % 2 == 0:
                    dve.wait_ge(x_loaded[t // 2], 16)
                if t >= 2:
                    dve.wait_ge(tr_done, tr_x(t - 2) + 1)
                normalise(t, resid[:, t, :], xn[:, t % 2, :], xn_ready)

            def x_low(k, t):
                cols = slice(t * P, (t + 1) * P)
                tr_low(k, xnT[:, 1, :, cols], blocks(k), xnT[:, 0, :, cols])

            def memory_wq(m):
                tr_low(tr_wqa(m), wqaT[:, 1, m, :, :], blocks(tr_wqa(m)), wqaT[:, 0, m, :, :])

            norm_x(0)
            norm_x(1)
            dve.wait_ge(tr_done, TR_BZ + 1)
            settled(nc.vector.tensor_copy(bz[:, :], tr_bank(TR_BZ)[:, 0:2 * MH]))
            nc.vector.tensor_scalar(neg_bq[:, :], bz[:, 0:MH], -1.0, None, ALU.mult).then_inc(tr_used, 1)
            for i in range(NT):
                if i + 2 < NT:
                    norm_x(i + 2)
                if i == 0:
                    x_low(tr_x(0), 0)
                if i + 1 < NT:
                    x_low(tr_x(i + 1), i + 1)
                if i:
                    memory_wq(i - 1)
                if i == NT - 1:
                    memory_wq(i)

            def memory_head(i):
                if 1 <= i <= 2 * MH:
                    dve.wait_ge(den_done, i)
                    if i >= 3:
                        dve.wait_ge(spread_done, i - 2)
                    r = rden[:, (i - 1) % 2, :]
                    settled(nc.vector.tensor_scalar(r, den_bank[:, 0:4], DEN_EPS, None, ALU.add))
                    nc.vector.reciprocal(r, r).then_inc(rden_ready, 1)
                if 1 <= i <= MH:
                    k = mm_memwo(i - 1)
                    dve.wait_ge(mm_act, k + 1)
                    low(memwo[:, 1, i - 1, :], mm_bank(k)[:, :], memwo[:, 0, i - 1, :]).then_inc(mm_dve, 1)
                if i >= 2:
                    old = sig[:, (i - 2) % 3, :]
                    dve.wait_ge(spread_done, i - 1)
                    nc.vector.tensor_tensor(old, old, spread_bank(i - 2)[:, :], ALU.mult)\
                        .then_inc(sig_scaled, 1)
                if i < 2 * MH:
                    dve.wait_ge(mm_act, mm_query(i) + 1)
                    dve.wait_ge(qexp_ready, i + 1)
                    nc.vector.tensor_tensor(sig[:, i % 3, :], qneg[:, :], qpos[:, :], ALU.add)\
                        .then_inc(sig_ready, 1)
                if i < MH:
                    k = tr_mem(i)
                    tr_low(k, memT[:, 1, :], tr_bank(k)[:, 0:P], memT[:, 0, :])
                    tr_low(k + 1, wofT[:, 1, :], tr_bank(k + 1)[:, :], wofT[:, 0, :])
                if i >= 2:
                    dve.wait_ge(sig_hi, i - 1)
                    low(sigT[:, 1, (i - 2) % MH, :], old, sigT[:, 0, (i - 2) % MH, :]).then_inc(sig_lo, 1)

            for i in range(MH + 2):
                memory_head(i)

            def add_memory(t):
                dve.wait_ge(y_done, t + 1)
                nc.vector.tensor_tensor(resid[:, t, :], resid[:, t, :], y_bank(t)[:, :], ALU.add)\
                    .then_inc(y_used, 1)
                dve.wait_ge(y_used, t + 1)
                if t >= 2:
                    dve.wait_ge(tr_done, TR_X2 + t - 1)
                normalise(NT + t, resid[:, t, :], xn[:, t % 2, :], xn_ready)

            for t in range(4):
                add_memory(t)
                if t:
                    x_low(TR_X2 + t - 1, t - 1)
            for i in range(MH + 2, 2 * MH + 2):
                memory_head(i)
                if i == MH + 3:
                    x_low(TR_X2 + 3, 3)
            for t in range(4, NT):
                add_memory(t)
                if t > 4:
                    x_low(TR_X2 + t - 1, t - 1)
                if t < 6:
                    wkv_low(t - 4, wkv2, (t - 2) * KC)
            x_low(TR_X2 + 7, 7)

            def wq_low(g, j):
                dve.wait_ge(wq_hi, 4 * g + j + 1)
                low(wq[:, 1, 2 * j:2 * j + 2, :, :], wq_raw[:, :, :].rearrange("p k (h n) -> p h k n", h=2),
                    wq[:, 0, 2 * j:2 * j + 2, :, :]).then_inc(wq_lo, 1)

            def v_low(g, t):
                dve.wait_ge(v_hi, 8 * g + t + 1)
                low(v_ring[:, t % 2, :, 1, :], v_raw[:, t % 2, :, :], v_ring[:, t % 2, :, 0, :]).then_inc(v_lo, 1)

            def wo_low(g, h):
                dve.wait_ge(wo_hi, 8 * g + h + 1)
                low(wo[:, 1, h, :], wo_raw[:, h, :], wo[:, 0, h, :]).then_inc(wo_lo, 1)

            for j in range(4):
                wq_low(0, j)
            for h in range(GH):
                wo_low(0, h)
                if h == 5:
                    v_low(0, 0)
            nc.vector.tensor_copy(stats[:, 0:1], meanvar[:, 0:1]).then_inc(proj_added, 1)

            def save_router():
                dve.wait_ge(routT_done, 1)
                nc.vector.tensor_copy(routT, bank[5][:, 0:KC * NE].rearrange("p (k n) -> p k n", k=KC))\
                    .then_inc(routT_ready, 1)

            def expert_norm(e):
                dve.wait_ge(proj_added, 8 * (KV - 1) + e + 2)
                if e == NT - 1:
                    dve.wait_ge(pT_done, 2 * KV * NT)
                elif e >= 2:
                    dve.wait_ge(e_tr_done, e - 1)
                    dve.wait_ge(e_out_ready, e - 1)
                normalise(2 * NT + e, resid[:, e, :], e_xn_of(e), e_xn_ready)

            def expert_max(e):
                r = e % 2
                logits = small[:, r, 0, :]
                dve.wait_ge(logits_done, e + 1)
                nc.vector.tensor_tensor(logits, bank[5][:, 0:NE], rout_b, ALU.add).then_inc(logits_saved, 1)
                dve.wait_ge(logits_saved, e + 1)
                settled(nc.vector.max(top[:, r, 0, :], logits))
                nc.vector.tensor_scalar(top[:, r, 1, 0:1], top[:, r, 0, 0:1], -1.0, None, ALU.mult)\
                    .then_inc(e_max_ready, 1)

            def expert_top(e):
                r = e % 2
                expd, score, rest, weight = (small[:, r, i, :] for i in range(1, 5))
                dve.wait_ge(e_exp_done, e + 1)
                settled(nc.vector.reciprocal(top[:, r, 2, 1:2], top[:, r, 2, 0:1]))
                settled(nc.vector.tensor_scalar(score, expd, top[:, r, 2, 1:2], None, ALU.mult))
                settled(nc.vector.max(top[:, r, 3, :], score))
                nc.vector.tensor_reduce(top[:, r, 2, 2:3], top[:, r, 3, :], axis=AX, op=ALU.add)
                settled(nc.vector.match_replace(rest, top[:, r, 3, :], score, 0.0))
                nc.vector.tensor_tensor(weight, score, rest, ALU.subtract).then_inc(e_w_ready, 1)

            def scale_expert(e):
                if 2 <= e < NT - 1:
                    dve.wait_ge(out_written[e % 2], 16 * (e // 2))
                nc.vector.scalar_tensor_tensor(out=e_out_of(e), in0=e_xn_of(e),
                                               scalar=top[:, e % 2, 2, 2:3], in1=resid[:, e, :],
                                               op0=ALU.mult, op1=ALU.add).then_inc(e_scaled, 1)

            def add_mix(e):
                dve.wait_ge(e_scaled, e + 1)
                dve.wait_ge(mix_done, e + 1)
                nc.vector.tensor_tensor(e_out_of(e), e_out_of(e), bank[e_banks(e)[1]][:, :], ALU.add)\
                    .then_inc(e_out_ready, 1)

            def step(g, t, last_group, first_step=False):
                n = 8 * g + t
                for bb in range(2):
                    dve.wait_ge(scores_done, 2 * n + bb + 1)
                    nc.vector.tensor_reduce(negmax[:, bb, :], bank[bb][:, :].rearrange("p (c n) -> p c n", c=4),
                                            axis=AX, op=ALU.max, negate=True).then_inc(negmax_ready, 1)
                if last_group and t >= 2:
                    expert_norm(t - 2)
                for bb in range(2):
                    dve.wait_ge(exp_done, 2 * n + bb + 1)
                    nc.vector.reciprocal(rrow[:, bb, :], rowsum[:, bb, :]).then_inc(rrow_ready, 1)
                    dve.wait_ge(rrow_ready, 2 * n + bb + 1)
                    nc.vector.tensor_tensor(probs[:, bb, :, :], probs[:, bb, :, :],
                                            rrow[:, bb, :].unsqueeze(2).broadcast_to([P, 4, P]),
                                            ALU.mult).then_inc(probs_ready, 1)
                if not (last_group and t == 7):
                    v_low(g, t + 1)
                if not last_group and 2 <= t <= 5:
                    wq_low(g + 1, t - 2)
                if t == 0 and not first_step:
                    for h in range(GH):
                        wo_low(g, h)
                if not first_step:
                    dve.wait_ge(proj_done, n)
                    rows = resid[:, (t - 1) % NT, :]
                    nc.vector.tensor_tensor(rows, rows, bank[7][:, :], ALU.add).then_inc(proj_added, 1)
                for bb in range(2):
                    dve.wait_ge(pT_hi, 2 * n + bb + 1)
                    low(pT[:, bb, 1, :], bank[2 + bb][:, :], pT[:, bb, 0, :]).then_inc(pT_lo, 1)
                if last_group and t == 1:
                    save_router()
                if last_group and t >= 2:
                    expert_max(t - 2)
                if last_group and t >= 3:
                    scale_expert(t - 3)
                    add_mix(t - 3)
                for bb in range(2):
                    dve.wait_ge(oT_hi, 2 * n + bb + 1)
                    cols = slice(bb * S, (bb + 1) * S)
                    low(oT[:, t % 2, 1, :, cols], bank[4 + bb][:, :].rearrange("p (h s) -> p h s", h=GH),
                        oT[:, t % 2, 0, :, cols]).then_inc(oT_lo, 1)
                if last_group and t == NT - 1:
                    expert_norm(t - 1)
                if last_group and t >= 2:
                    expert_top(t - 2)

            step(0, 0, False, True)
            with dve.Fori(0, KV - 1) as g:
                for t in range(1, NT):
                    step(g, t, False)
                step(g + 1, 0, False)
            for t in range(1, NT):
                step(KV - 1, t, True)
            dve.wait_ge(proj_done, KV * NT)
            nc.vector.tensor_tensor(resid[:, NT - 1, :], resid[:, NT - 1, :], bank[7][:, :], ALU.add)\
                .then_inc(proj_added, 1)
            expert_norm(NT - 1)
            expert_max(NT - 2)
            scale_expert(NT - 3)
            expert_top(NT - 2)
            expert_max(NT - 1)
            add_mix(NT - 3)
            scale_expert(NT - 2)
            expert_top(NT - 1)
            add_mix(NT - 2)
            scale_expert(NT - 1)
            add_mix(NT - 1)


_INS = ["x", "ctx_4096", "L0_attn_Wq", "L0_attn_bq", "L0_attn_Wo", "L0_attn_M", "L0_attn_z",
        "L0_xattn_Wq", "L0_xattn_Wk", "L0_xattn_Wv", "L0_xattn_Wo",
        "L0_ffn_router_weight", "L0_ffn_router_bias", "L0_ffn_expert_bias"]


def kernel(**inputs):
    import numpy as _np
    import concourse.bacc as _bacc
    from concourse import mybir as _mybir
    from concourse.bass_utils import run_bass_kernel_spmd as _run

    nc = _bacc.Bacc("TRN2", target_bir_lowering=False, num_devices=1)
    arrays, args = {}, []
    for name in _INS:
        a = _np.ascontiguousarray(inputs[name])
        arrays[f"in_{name}"] = a
        args.append(nc.dram_tensor(f"in_{name}", a.shape, _mybir.dt.from_np(a.dtype), kind="ExternalInput").ap())
    shape = inputs["x"].shape
    args.append(nc.dram_tensor("out_x", shape, _mybir.dt.float32, kind="ExternalOutput").ap())
    decoder_layer(nc, *args)
    r = _run(nc, [arrays], core_ids=[0])
    return r.results[0]["out_x"]
```
